# Optimizing a Trainium2 kernel written in Bass

```python
import numpy as np
import jax
import jax.numpy as jnp

def _softmax(x, axis=-1):
    return jax.nn.softmax(x, axis=axis)

def _gelu(x):
    return jax.nn.gelu(x, approximate=True)

def _silu(x):
    return jax.nn.silu(x)

def _sigmoid(x):
    return jax.nn.sigmoid(x)

def _layernorm(x, axis=-1, eps=1e-05):
    m = jnp.mean(x, axis=axis, keepdims=True)
    v = jnp.var(x, axis=axis, keepdims=True)
    return (x - m) / jnp.sqrt(v + eps)

def _scatter_add(tgt, idx, src, axis=0):
    return tgt.at[idx].add(src)

def _segment_sum(src, seg, n):
    return jax.ops.segment_sum(src, seg, n)
kernel_name = 'mk_adj_ffn_d1_adj_r2_58df77'

def setup_inputs(seed: int=0):
    np.random.seed(seed)
    _w = jnp.asarray

    def _rec_inputs():
        import jax
        import jax.numpy as jnp
        _gk = jax.random.key(seed)
        x = -0.001003 + 1 * jax.random.normal(jax.random.fold_in(_gk, 1), (3327, 256), jnp.float32)
        _a = jax.random.bernoulli(jax.random.fold_in(_gk, 2), 0.00961827, (3327, 3327))
        _a = jnp.logical_or(_a, jnp.eye(3327, dtype=bool))
        _af = _a.astype(jnp.float32)
        adj = _af
        return (x, adj)
    x, adj = _rec_inputs()

    def _L0_gnn_setup():
        import jax, jax.numpy as jnp
        import numpy as np
        N, F, H = (1536, 256, 4)
        D = F // H
        ALPHA = 0.5
        EPS = 1e-06

        def _batchnorm(x, gamma, beta):
            m = jnp.mean(x, axis=0)
            v = jnp.var(x, axis=0)
            return (x - m) * jax.lax.rsqrt(v + EPS) * gamma + beta

        def _masked_softmax(scores, mask):
            s = jnp.where(mask, scores, -jnp.inf)
            att = jax.nn.softmax(s, axis=-1)
            return jnp.where(mask, att, 0.0)

        def _mlp_block(x, Wm, bm, g, b):
            h = jax.nn.elu(x @ Wm.T + bm) + x
            return _batchnorm(h, g, b)
        key = jax.random.key(seed)
        ks = jax.random.split(key, 12)
        X = jax.random.normal(ks[0], (N, F), dtype=jnp.float32)
        eye = jnp.eye(N, dtype=jnp.float32)
        local = (jax.random.uniform(ks[1], (N, N)) < 32.0 / N).astype(jnp.float32)
        local = jnp.clip(local + eye, 0.0, 1.0)
        longr = (jax.random.uniform(ks[2], (N, N)) < 16.0 / N).astype(jnp.float32)
        longr = jnp.clip(longr + eye, 0.0, 1.0)
        W = jax.random.normal(ks[3], (H, D, D), dtype=jnp.float32) * 0.1
        V = jax.random.normal(ks[4], (H, 2, D, 1), dtype=jnp.float32) * 0.1
        return {'X': X, 'local_pattern': local, 'long_range_pattern': longr, 'W': W, 'V': V, 'enc_bn_gamma': jnp.ones((F,), jnp.float32), 'enc_bn_beta': jnp.zeros((F,), jnp.float32), 'enc_mlp_W': jax.random.normal(ks[5], (F, F), dtype=jnp.float32) * 0.02, 'enc_mlp_b': jnp.zeros((F,), jnp.float32), 'enc_mlp_bn_gamma': jnp.ones((F,), jnp.float32), 'enc_mlp_bn_beta': jnp.zeros((F,), jnp.float32), 'dec_mlp_W': jax.random.normal(ks[6], (F, F), dtype=jnp.float32) * 0.02, 'dec_mlp_b': jnp.zeros((F,), jnp.float32), 'dec_mlp_bn_gamma': jnp.ones((F,), jnp.float32), 'dec_mlp_bn_beta': jnp.zeros((F,), jnp.float32)}
    _L0_gnn_all = _L0_gnn_setup()
    _L0_gnn_in = {k: v for k, v in _L0_gnn_all.items() if k in ('W', 'V', 'enc_bn_gamma', 'enc_bn_beta', 'enc_mlp_W', 'enc_mlp_b', 'enc_mlp_bn_gamma', 'enc_mlp_bn_beta', 'dec_mlp_W', 'dec_mlp_b', 'dec_mlp_bn_gamma', 'dec_mlp_bn_beta')}
    del _L0_gnn_all

    def _L0_ffn_setup():
        import jax, jax.numpy as jnp
        import numpy as np
        D_MODEL = 256
        N_EXPERTS = 8
        D_FF = 1024
        TOP_K = 2
        B, S = (2, 1024)
        key = jax.random.key(seed)
        ks = jax.random.split(key, 4)
        init = lambda k, shape, fan_in: jax.random.normal(k, shape, jnp.float32) / np.float32(np.sqrt(fan_in))
        return {'x': jax.random.normal(ks[0], (B, S, D_MODEL), jnp.float32), 'Wg': init(ks[1], (D_MODEL, N_EXPERTS), D_MODEL), 'bg': jnp.zeros((N_EXPERTS,), jnp.float32), 'W1': init(ks[2], (N_EXPERTS, D_MODEL, D_FF), D_MODEL), 'b1': jnp.zeros((N_EXPERTS, D_FF), jnp.float32), 'W2': init(ks[3], (N_EXPERTS, D_FF, D_MODEL), D_FF), 'b2': jnp.zeros((N_EXPERTS, D_MODEL), jnp.float32)}
    _L0_ffn_all = _L0_ffn_setup()
    _L0_ffn_in = {k: v for k, v in _L0_ffn_all.items() if k in ('Wg', 'bg', 'W1', 'b1', 'W2', 'b2')}
    del _L0_ffn_all
    return {'x': x, 'adj': adj, 'L0_gnn_W': _L0_gnn_in['W'], 'L0_gnn_V': _L0_gnn_in['V'], 'L0_gnn_enc_bn_gamma': _L0_gnn_in['enc_bn_gamma'], 'L0_gnn_enc_bn_beta': _L0_gnn_in['enc_bn_beta'], 'L0_gnn_enc_mlp_W': _L0_gnn_in['enc_mlp_W'], 'L0_gnn_enc_mlp_b': _L0_gnn_in['enc_mlp_b'], 'L0_gnn_enc_mlp_bn_gamma': _L0_gnn_in['enc_mlp_bn_gamma'], 'L0_gnn_enc_mlp_bn_beta': _L0_gnn_in['enc_mlp_bn_beta'], 'L0_gnn_dec_mlp_W': _L0_gnn_in['dec_mlp_W'], 'L0_gnn_dec_mlp_b': _L0_gnn_in['dec_mlp_b'], 'L0_gnn_dec_mlp_bn_gamma': _L0_gnn_in['dec_mlp_bn_gamma'], 'L0_gnn_dec_mlp_bn_beta': _L0_gnn_in['dec_mlp_bn_beta'], 'L0_ffn_Wg': _L0_ffn_in['Wg'], 'L0_ffn_bg': _L0_ffn_in['bg'], 'L0_ffn_W1': _L0_ffn_in['W1'], 'L0_ffn_b1': _L0_ffn_in['b1'], 'L0_ffn_W2': _L0_ffn_in['W2'], 'L0_ffn_b2': _L0_ffn_in['b2']}

def reference(x, adj, L0_gnn_W, L0_gnn_V, L0_gnn_enc_bn_gamma, L0_gnn_enc_bn_beta, L0_gnn_enc_mlp_W, L0_gnn_enc_mlp_b, L0_gnn_enc_mlp_bn_gamma, L0_gnn_enc_mlp_bn_beta, L0_gnn_dec_mlp_W, L0_gnn_dec_mlp_b, L0_gnn_dec_mlp_bn_gamma, L0_gnn_dec_mlp_bn_beta, L0_ffn_Wg, L0_ffn_bg, L0_ffn_W1, L0_ffn_b1, L0_ffn_W2, L0_ffn_b2):
    import jax
    import jax.numpy as jnp

    def _L0_gnn_ref(X, local_pattern, long_range_pattern, W, V, enc_bn_gamma, enc_bn_beta, enc_mlp_W, enc_mlp_b, enc_mlp_bn_gamma, enc_mlp_bn_beta, dec_mlp_W, dec_mlp_b, dec_mlp_bn_gamma, dec_mlp_bn_beta):
        import jax, jax.numpy as jnp
        import numpy as np
        N, F, H = (1536, 256, 4)
        D = F // H
        ALPHA = 0.5
        EPS = 1e-06

        def _batchnorm(x, gamma, beta):
            m = jnp.mean(x, axis=0)
            v = jnp.var(x, axis=0)
            return (x - m) * jax.lax.rsqrt(v + EPS) * gamma + beta

        def _masked_softmax(scores, mask):
            s = jnp.where(mask, scores, -jnp.inf)
            att = jax.nn.softmax(s, axis=-1)
            return jnp.where(mask, att, 0.0)

        def _mlp_block(x, Wm, bm, g, b):
            h = jax.nn.elu(x @ Wm.T + bm) + x
            return _batchnorm(h, g, b)
        n = X.shape[0]
        Xh = X.reshape(n, H, D).transpose(1, 0, 2)
        Xw = jnp.einsum('hnd,hde->hne', Xh, W)
        f1 = jnp.einsum('hnd,hd->hn', Xw, V[:, 0, :, 0])
        f2 = jnp.einsum('hnd,hd->hn', Xw, V[:, 1, :, 0])
        sig = jax.nn.sigmoid(f1[:, :, None] + f2[:, None, :])
        lmask = (local_pattern != 0)[None]
        gmask = (long_range_pattern != 0)[None]
        local_att = _masked_softmax(local_pattern[None] * sig, lmask)
        long_att = _masked_softmax(long_range_pattern[None] * sig, gmask)
        att = ALPHA * long_att + (1.0 - ALPHA) * local_att
        Xa = jnp.einsum('hij,hjd->hid', att, Xw)
        Xc = Xa.transpose(1, 0, 2).reshape(n, F)
        Xn = _batchnorm(Xc, enc_bn_gamma, enc_bn_beta)
        emb = _mlp_block(Xn, enc_mlp_W, enc_mlp_b, enc_mlp_bn_gamma, enc_mlp_bn_beta)
        Yh = emb.reshape(n, H, D).transpose(1, 0, 2)
        Y = jnp.einsum('hij,hjd->hid', att, Yh)
        Y = jnp.einsum('hnd,hed->hne', Y, W)
        Yc = Y.transpose(1, 0, 2).reshape(n, F)
        Yc = jax.nn.elu(Yc)
        out = _mlp_block(Yc, dec_mlp_W, dec_mlp_b, dec_mlp_bn_gamma, dec_mlp_bn_beta)
        return out

    def _L0_ffn_ref(x, Wg, bg, W1, b1, W2, b2):
        import jax, jax.numpy as jnp
        import numpy as np
        D_MODEL = 256
        N_EXPERTS = 8
        D_FF = 1024
        TOP_K = 2
        B, S = (2, 1024)
        b, s, d = x.shape
        xt = x.reshape(-1, d)
        logits = xt @ Wg + bg
        probs = jax.nn.softmax(logits, axis=-1)
        top_p, top_i = jax.lax.top_k(probs, TOP_K)
        top_p = top_p / top_p.sum(axis=-1, keepdims=True)
        T = xt.shape[0]
        combine = jnp.zeros((T, N_EXPERTS), x.dtype).at[jnp.arange(T)[:, None], top_i].add(top_p)
        h = jax.nn.relu(jnp.einsum('td,edf->etf', xt, W1) + b1[:, None, :])
        y = jnp.einsum('etf,efd->etd', h, W2) + b2[:, None, :]
        out = jnp.einsum('te,etd->td', combine, y)
        return out.reshape(b, s, d)
    x = x + _L0_gnn_ref(_layernorm(x, axis=-1), adj, adj, L0_gnn_W, L0_gnn_V, L0_gnn_enc_bn_gamma, L0_gnn_enc_bn_beta, L0_gnn_enc_mlp_W, L0_gnn_enc_mlp_b, L0_gnn_enc_mlp_bn_gamma, L0_gnn_enc_mlp_bn_beta, L0_gnn_dec_mlp_W, L0_gnn_dec_mlp_b, L0_gnn_dec_mlp_bn_gamma, L0_gnn_dec_mlp_bn_beta)
    x = x + _L0_ffn_ref(_layernorm(x, axis=-1)[None], L0_ffn_Wg, L0_ffn_bg, L0_ffn_W1, L0_ffn_b1, L0_ffn_W2, L0_ffn_b2)[0]
    return x

_drawn_inputs = setup_inputs


def setup_inputs(seed=0):
    import zlib

    import numpy as np

    out = dict(_drawn_inputs(seed))
    spreads = {'L0_gnn_enc_bn_gamma': (1.0, 0.2),
     'L0_gnn_enc_bn_beta': (0.0, 1.396),
     'L0_gnn_enc_mlp_b': (0.0, 0.34),
     'L0_gnn_enc_mlp_bn_gamma': (1.0, 0.2),
     'L0_gnn_enc_mlp_bn_beta': (0.0, 0.1),
     'L0_gnn_dec_mlp_b': (0.0, 0.1),
     'L0_gnn_dec_mlp_bn_gamma': (1.0, 0.2),
     'L0_gnn_dec_mlp_bn_beta': (0.0, 0.1),
     'L0_ffn_bg': (0.0, 0.1),
     'L0_ffn_b1': (0.0, 0.1),
     'L0_ffn_b2': (0.0, 0.1)}
    factors = {}
    for name, (base, spread) in spreads.items():
        noise = np.random.default_rng([zlib.crc32(name.encode()), seed]).standard_normal(out[name].shape)
        drawn = base * np.exp(spread * noise) if base else spread * noise
        out[name] = jnp.asarray(drawn.astype(out[name].dtype))
    for name, factor in factors.items():
        out[name] = (out[name] * factor).astype(out[name].dtype)
    return out
```

```python
from contextlib import ExitStack

import concourse.bass as bass
from concourse import mybir

F32 = mybir.dt.float32
U8 = mybir.dt.uint8
U32 = mybir.dt.uint32
ALU = mybir.AluOpType
ACT = mybir.ActivationFunctionType

P = 128
N = 3327
T = -(-N // P)
NP = T * P
F = 256
KT = F // P
H = 4
D = F // H
HALF = NP // 2
NB = 4
BLK = HALF // NB
BLOCKS = 2 * NB
PASSES = 4
E = 8
FF = 1024
FT = FF // P
TB = 2
FB = T // TB
LN_EPS = 1e-5
BN_EPS = 1e-6
TINY = 1e-30
AHEAD = 2


def build(nc, x, adj_t, w, wt, v, enc_g, enc_b, emw_t, emb, em_g, em_b, dmw_t, dmb, dm_g, dm_b,
          wg, bg, w1, b1, w2, b2, out):
    xw_dram = nc.dram_tensor("xw_scratch", [NP, F], F32, kind="Internal").ap()
    f1_dram = nc.dram_tensor("f1_scratch", [H, NP], F32, kind="Internal").ap()
    inv_dram = nc.dram_tensor("inv_scratch", [2 * PASSES, 2, HALF], F32, kind="Internal").ap()

    with ExitStack() as ctx:
        def sb(name, shape, dt=F32, scope=ctx):
            return scope.enter_context(nc.sbuf_tensor(name, shape, dt))

        def sem(name):
            return ctx.enter_context(nc.semaphore(name))

        ident = sb("ident", [P, P])
        w_bd = sb("w_bd", [P, KT, P])
        wt_bd = sb("wt_bd", [P, KT, P])
        v_bd = sb("v_bd", [P, KT, 2 * H])
        wv = sb("wv", [P, KT, 2 * H])
        emw_sb = sb("emw_sb", [P, KT, F])
        dmw_sb = sb("dmw_sb", [P, KT, F])
        vecs = sb("vecs", [P, 8, KT])
        ENC_G, ENC_B, EMB, EM_G, EM_B, DMB, DM_G, DM_B = range(8)
        bg_sb = sb("bg_sb", [P, E])
        wg_sb = sb("wg_sb", [P, KT, E])
        b1_sb = sb("b1_sb", [P, E, FT])
        b2_sb = sb("b2_sb", [E, F])
        f2h = sb("f2h", [P, T * H])
        stats = sb("stats", [P, T, 6])
        mv = sb("mv", [P, T, 2])
        rstd = sb("rstd", [P, T])
        bnst = sb("bnst", [P, KT, BLOCKS, 6])
        bnmv = sb("bnmv", [P, KT, 2])
        bnsc = sb("bnsc", [P, KT, 4])
        den = sb("den", [P, 2 * HALF // P])
        eiota = sb("eiota", [P, E], U32)
        eidx = sb("eidx", [P, E])
        comb_t = sb("comb_t", [E, P * 2])

        buf_s = sb("buf_s", [P, 2, NP])
        buf_p = sb("buf_p", [P, 2, NP])
        buf_e = sb("buf_e", [P, 2, NP])
        xc = sb("xc", [P, KT, NP])
        stage = sb("stage", [P, 2, 3 * D])

        with ExitStack() as attn:
            mask = sb("mask", [P, T, HALF], U8, attn)
            f1b = sb("f1b", [P, 2, 2, HALF], F32, attn)
            raw = sb("raw", [P, 2, HALF], F32, attn)
            invb = sb("invb", [P, HALF], F32, attn)
        x1 = sb("x1", [P, T, F])
        w1_sb = sb("w1_sb", [P, 2, KT, FF])
        w2_sb = sb("w2_sb", [P, 2, FT, F])
        h_sb = sb("h_sb", [P, FT, TB * P])
        logits = sb("logits", [P, T, E])
        top = sb("top", [P, T, 8])
        topi = sb("topi", [P, T, 8], U32)
        topf = sb("topf", [P, T, 2])
        gate = sb("gate", [P, T, 4])
        hot = sb("hot", [P, 2, T, E])
        comb = sb("comb", [P, T, E])

        ps = ctx.enter_context(nc.psum_tensor("ps", [P, 8, 512], F32))

        x_loaded = [sem(f"x_loaded{i}") for i in range(2)]
        consts_loaded = sem("consts_loaded")
        zeroed = sem("zeroed")
        ident_made = sem("ident_made")
        wv_made = sem("wv_made")
        wv_copied = sem("wv_copied")
        dve_step = sem("dve_step")
        var_ready = sem("var_ready")
        std_ready = sem("std_ready")
        ln_done = sem("ln_done")
        tr_done = sem("tr_done")
        tr_copied = sem("tr_copied")
        xw_done = sem("xw_done")
        xw_copied = sem("xw_copied")
        f1_done = sem("f1_done")
        f1_copied = sem("f1_copied")
        f1_stored = sem("f1_stored")
        xw_stored = sem("xw_stored")
        f1b_loaded = [sem(f"f1b_loaded{i}") for i in range(2)]
        stage_loaded = [sem(f"stage_loaded{i}") for i in range(2)]
        mask_loaded = [sem(f"mask_loaded{i}") for i in range(2)]
        tanh_done = sem("tanh_done")
        exp_done = sem("exp_done")
        masked = sem("masked")
        multiplied = sem("multiplied")
        e_free = sem("e_free")
        bank_done = sem("bank_done")
        raw_copied = sem("raw_copied")
        den_moved = sem("den_moved")
        inv_ready = sem("inv_ready")
        inv_stored = sem("inv_stored")
        inv_spread = sem("inv_spread")
        xc_ready = sem("xc_ready")
        bn_applied = sem("bn_applied")
        z_done = sem("z_done")
        elu_exp = sem("elu_exp")
        elu_relu = sem("elu_relu")
        h_done = sem("h_done")
        emb_done = sem("emb_done")
        et_done = sem("et_done")
        et_copied = sem("et_copied")
        emb_stored = sem("emb_stored")
        res_loaded = sem("res_loaded")
        ot_done = sem("ot_done")
        x1_done = sem("x1_done")
        ln2_done = sem("ln2_done")
        tr2_done = sem("tr2_done")
        tr2_copied = sem("tr2_copied")
        lg_done = sem("lg_done")
        gate_exp = sem("gate_exp")
        gate_in = sem("gate_in")
        comb_done = sem("comb_done")
        ct_done = sem("ct_done")
        ct_copied = sem("ct_copied")
        b2_done = sem("b2_done")
        b2_added = sem("b2_added")
        w_loaded = [sem(f"w_loaded{i}") for i in range(2)]
        up_done = sem("up_done")
        relu_done = sem("relu_done")
        down_done = sem("down_done")
        y_added = sem("y_added")
        out_stored = sem("out_stored")

        NCONST = 0
        xtm = buf_s[:, :, :].rearrange("p a n -> p (a n)").rearrange("p (t f) -> p t f", f=F)
        ptm = buf_p[:, :, :].rearrange("p a n -> p (a n)").rearrange("p (t f) -> p t f", f=F)
        f1row = raw[0:H, :, :].rearrange("p a n -> p (a n)")
        x_tm = x.rearrange("(t p) f -> p t f", p=P)
        T0 = T // 2

        consts = []
        for h in range(H):
            q = slice((h % 2) * D, (h % 2) * D + D)
            consts.append((w_bd[q, h // 2, q], w[h]))
            consts.append((wt_bd[q, h // 2, q], wt[h]))
            for k in range(2):
                consts.append((v_bd[q, h // 2, H * k + h:H * k + h + 1], v[h, k]))
        for n, a in enumerate((enc_g, enc_b, emb, em_g, em_b, dmb, dm_g, dm_b)):
            consts.append((vecs[:, n, :], a.rearrange("(t p) -> p t", p=P)))
        consts += [(emw_sb[:, :, :], emw_t.rearrange("(t p) o -> p t o", p=P)),
                   (dmw_sb[:, :, :], dmw_t.rearrange("(t p) o -> p t o", p=P)),
                   (wg_sb[:, :, :], wg.rearrange("(t p) e -> p t e", p=P)),
                   (b1_sb[:, :, :], b1.rearrange("e (t p) -> p e t", p=P)),
                   (b2_sb[:, :], b2),
                   (bg_sb[:, :], bg.rearrange("(a e) -> a e", a=1).to_broadcast([P, E]))]
        ALL_CONSTS = 16 * len(consts)
        STEPS = T * PASSES
        UNITS = KT * BLOCKS

        block = ctx.enter_context(nc.Block())

        @block.sync
        def _(sp):
            for i in range(2):
                sp.dma_start(xtm[:, i * T0:(i + 1) * T0, :], x_tm[:, i * T0:(i + 1) * T0, :]).then_inc(x_loaded[i], 16)
            sp.wait_ge(zeroed, 3)
            with nc.allow_non_contiguous_dma(reason="small vectors"):
                for dst, src in consts:
                    sp.dma_start(dst, src).then_inc(consts_loaded, 16)
            sp.wait_ge(xw_copied, T)
            sp.dma_start(xw_dram.rearrange("(t p) f -> p t f", p=P), ptm).then_inc(xw_stored, 16)
            sp.wait_ge(f1_copied, BLOCKS)
            sp.dma_start(f1_dram, f1row).then_inc(f1_stored, 16)

            def load_f1(gp):
                half, pair = gp % PASSES // 2, gp % 2
                if gp >= 2:
                    sp.wait_ge(tanh_done, 2 * T * (gp - 1))
                src = f1_dram[2 * pair:2 * pair + 2, half * HALF:(half + 1) * HALF]
                sp.dma_start(f1b[:, gp % 2, :, :], src.rearrange("(a h) n -> a h n", a=1).to_broadcast([P, 2, HALF])) \
                    .then_inc(f1b_loaded[gp % 2], 16)

            sp.wait_ge(f1_stored, 16)
            load_f1(0)
            sp.wait_ge(xw_stored, 16)
            for gp in range(2 * PASSES):
                pair = gp % 2
                if gp + 1 < 2 * PASSES:
                    load_f1(gp + 1)
                if gp == PASSES:
                    sp.wait_ge(emb_stored, 16)
                with sp.Fori(0, T // 2) as t:
                    for s in range(2):
                        sp.wait_ge(e_free, gp * T + t * 2 + s + 1)
                        sp.dma_start(
                            stage[:, s, :].rearrange("p (c d) -> p c d", d=D)[:, 0:3:2, :],
                            xw_dram[bass.ds(t * (2 * P) + s * P, P), pair * P:(pair + 1) * P]
                            .rearrange("p (c d) -> p c d", d=D)).then_inc(stage_loaded[s], 16)
                if gp == PASSES - 1:
                    sp.wait_ge(et_copied, T // 2)
                    sp.dma_start(xw_dram.rearrange("(t p) f -> p t f", p=P), xtm).then_inc(emb_stored, 16)
            sp.wait_ge(masked, 2 * STEPS + AHEAD)
            sp.wait_ge(xc_ready, 4 * PASSES)
            sp.dma_start(x1[:, :, :], x_tm).then_inc(res_loaded, 16)

            def load_expert(e, s):
                sp.dma_start(w1_sb[:, s, :, :], w1[bass.ds(e, 1)].rearrange("a (t p) f -> p (a t) f", p=P)).then_inc(w_loaded[s], 16)
                sp.dma_start(w2_sb[:, s, :, :], w2[bass.ds(e, 1)].rearrange("a (t p) f -> p (a t) f", p=P)).then_inc(w_loaded[s], 16)

            load_expert(0, 0)
            load_expert(1, 1)
            with sp.Fori(1, E // 2) as e2:
                for s in range(2):
                    sp.wait_ge(down_done, e2 * (2 * FB) + ((s - 1) * FB + 1))
                    load_expert(e2 * 2 + s, s)
            sp.wait_ge(y_added, E * FB + 1)
            sp.dma_start(out[0:(T - 1) * P, :].rearrange("(t p) f -> p t f", p=P), x1[:, 0:T - 1, :]).then_inc(out_stored, 16)
            sp.dma_start(out[(T - 1) * P:N, :], x1[0:N - (T - 1) * P, T - 1, :]).then_inc(out_stored, 16)
            sp.wait_ge(out_stored, 32)

        @block.gpsimd
        def _(pool):
            nc.gpsimd.memset(w_bd[:, :, :], 0.0).then_inc(zeroed, 1)
            nc.gpsimd.memset(wt_bd[:, :, :], 0.0).then_inc(zeroed, 1)
            nc.gpsimd.memset(v_bd[:, :, :], 0.0).then_inc(zeroed, 1)
            nc.gpsimd.memset(ident[:, :], 0.0).then_inc(zeroed, 1)
            nc.gpsimd.memset(stage[:, :, :], 1.0).then_inc(zeroed, 1)
            nc.gpsimd.iota(eiota[:, :], [[1, E]], base=0, channel_multiplier=0).then_inc(zeroed, 1)
            pool.wait_ge(zeroed, 6)
            nc.gpsimd.tensor_copy(eidx[:, :], eiota[:, :]).then_inc(ident_made, 1)
            nc.gpsimd.affine_select(out=ident[:, :], in_=ident[:, :], compare_op=ALU.not_equal, fill=1.0,
                                    base=0, pattern=[[-1, P]], channel_multiplier=1).then_inc(ident_made, 1)

            def load_masks(count, half, after):
                def load_pair(t):
                    for s in range(2):
                        if after is not None:
                            pool.wait_ge(masked, t * 2 + (after + s + 1 + AHEAD))
                        if count or not isinstance(t, int):
                            pool.wait_ge(mask_loaded[s], (t + count * (T // 2)) * 16)
                        pool.dma_start(mask[:, bass.ds(t * 2 + s, 1), :].rearrange("p a n -> p (a n)"),
                                       adj_t[bass.ds(t * (2 * P) + s * P, P), half * HALF:(half + 1) * HALF]) \
                            .then_inc(mask_loaded[s], 16)

                load_pair(0)
                with pool.Fori(1, T // 2) as t:
                    load_pair(t)

            def spread_inverse(gp):
                pool.wait_ge(raw_copied, 2 * NB * (gp + 1))
                for h in range(2):
                    row = D * (1 - h)
                    pool.dma_start(den[:, h * (HALF // P):(h + 1) * (HALF // P)],
                                   raw[row:row + 1, h, :]).then_inc(den_moved, 16)
                pool.wait_ge(inv_ready, gp + 1)
                for h in range(2):
                    pool.dma_start(inv_dram[gp, h].rearrange("(p c) -> p c", p=P),
                                   den[:, h * (HALF // P):(h + 1) * (HALF // P)]).then_inc(inv_stored, 16)
                pool.wait_ge(inv_stored, 32 * (gp + 1))
                for h in range(2):
                    pool.dma_start(invb[h * D:(h + 1) * D, :],
                                   inv_dram[gp, h:h + 1].to_broadcast([D, HALF])).then_inc(inv_spread, 16)

            load_masks(0, 0, None)
            for gp in range(2 * PASSES):
                if gp:
                    spread_inverse(gp - 1)
                if gp % 2 and gp + 1 < 2 * PASSES:
                    load_masks((gp + 1) // 2, (gp // 2 + 1) % 2, gp * T)
            spread_inverse(2 * PASSES - 1)

        @block.scalar
        def _(act):
            act.sem_inc(exp_done, 1)
            act.wait_ge(var_ready, 1)
            nc.scalar.activation(rstd[:, :], rstd[:, :], ACT.Sqrt).then_inc(std_ready, 1)

            def copy_transposed(t, done, copied, dst):
                act.wait_ge(done, t + 1)
                nc.scalar.activation(dst[:, :, t * P:(t + 1) * P],
                                     ps[:, t % 4, 0:F].rearrange("p (k n) -> p k n", k=KT), ACT.Copy).then_inc(copied, 1)

            for t in range(T):
                copy_transposed(t, tr_done, tr_copied, buf_e)
            for b in range(BLOCKS):
                act.wait_ge(f1_done, b + 1)
                nc.scalar.activation(f1row[:, b * BLK:(b + 1) * BLK], ps[0:H, b % 4, 0:BLK], ACT.Copy).then_inc(f1_copied, 1)

            def tanh(gp, jt, s):
                act.wait_ge(exp_done, jt + gp * T if gp or not isinstance(jt, int) else max(jt, 1))
                for h in range(2):
                    col = jt * H + (gp % 2) * 2 + h
                    nc.scalar.activation(buf_s[:, s, h * HALF:(h + 1) * HALF], f1b[:, gp % 2, h, :], ACT.Tanh,
                                         bias=f2h[:, bass.ds(col, 1)], scale=0.5).then_inc(tanh_done, 1)

            def exp(step, s):
                act.wait_ge(tanh_done, step * 2 + 2)
                act.wait_ge(masked, step + 1)
                nc.scalar.activation(buf_p[:, s, :], buf_s[:, s, :], ACT.Exp, scale=0.5).then_inc(exp_done, 1)

            def attention(a):
                for q in range(PASSES):
                    gp = a * PASSES + q
                    g0 = gp * T
                    act.wait_ge(f1b_loaded[gp % 2], 16 * (gp // 2 + 1))
                    tanh(gp, 0, 0)
                    with act.Fori(0, T // 2 - 1) as t:
                        tanh(gp, t * 2 + 1, 1)
                        exp(t * 2 + g0, 0)
                        tanh(gp, t * 2 + 2, 0)
                        exp(t * 2 + (g0 + 1), 1)
                    tanh(gp, T - 1, 1)
                    exp(g0 + T - 2, 0)
                    exp(g0 + T - 1, 1)

            def bn_sqrt(n):
                act.wait_ge(var_ready, n + 1)
                nc.scalar.activation(bnsc[:, :, 0], bnsc[:, :, 0], ACT.Sqrt).then_inc(std_ready, 1)

            def elu_parts(base, bias):
                for u in range(UNITS):
                    m, b = u // BLOCKS, u % BLOCKS
                    cols = slice(b * BLK, (b + 1) * BLK)
                    act.wait_ge(z_done, base + u + 1)
                    z = ps[:, u % 8, 0:BLK]
                    bb = 0.0 if bias is None else vecs[:, bias, m:m + 1]
                    nc.scalar.activation(buf_s[:, m, cols], z, ACT.Exp, bias=bb).then_inc(elu_exp, 1)
                    nc.scalar.activation(buf_p[:, m, cols], z, ACT.Relu, bias=bb).then_inc(elu_relu, 1)

            act.wait_ge(xw_copied, T)
            act.wait_ge(xw_stored, 16)
            attention(0)
            bn_sqrt(1)
            elu_parts(0, EMB)
            bn_sqrt(2)
            for t in range(T // 2):
                act.wait_ge(et_done, t + 1)
                nc.scalar.activation(xtm[:, 2 * t:2 * t + 2, :], ps[:, t % 8, :].rearrange("p (t f) -> p t f", f=F),
                                     ACT.Copy).then_inc(et_copied, 1)
            act.wait_ge(emb_stored, 16)
            attention(1)
            elu_parts(UNITS, None)
            elu_parts(2 * UNITS, DMB)
            bn_sqrt(3)
            act.wait_ge(var_ready, 5)
            nc.scalar.activation(rstd[:, :], rstd[:, :], ACT.Sqrt).then_inc(std_ready, 1)
            for t in range(T):
                copy_transposed(t, tr2_done, tr2_copied, buf_e)
            act.wait_ge(gate_in, 1)
            nc.scalar.activation(gate[:, :, 1], gate[:, :, 0], ACT.Exp).then_inc(gate_exp, 1)
            with act.Fori(0, E) as e:
                with act.Fori(0, FB) as n:
                    for f in range(FT):
                        act.wait_ge(up_done, e * (FB * FT) + n * FT + (f // 2 * 2 + 2))
                        if f == 0:
                            act.wait_ge(down_done, e * FB + n + 1)
                        nc.scalar.activation(h_sb[:, f, :], ps[:, f // 2, (f % 2) * 256:(f % 2) * 256 + 256], ACT.Relu,
                                             bias=b1_sb[:, bass.ds(e, 1), f:f + 1].rearrange("p a b -> p (a b)")).then_inc(relu_done, 1)

        @block.vector
        def _(dve):
            steps = [0]

            def link(ins):
                steps[0] += 1
                ins.then_inc(dve_step, 1)
                dve.wait_ge(dve_step, steps[0])

            dve.sem_inc(masked, AHEAD)
            dve.sem_inc(y_added, 1)
            dve.wait_ge(consts_loaded, ALL_CONSTS)
            dve.wait_ge(ident_made, 2)

            def layer_norm(src, dst, n, done, loaded):
                for t in range(T):
                    if loaded is not None and t % T0 == 0:
                        dve.wait_ge(loaded[t // T0], 16)
                    last = nc.vector.bn_stats(stats[:, t, :], src[:, t, :])
                link(last)
                for t in range(T):
                    last = nc.vector.bn_aggr(mv[:, t, :], stats[:, t, :])
                link(last)
                nc.vector.tensor_scalar(rstd[:, :], mv[:, :, 1], LN_EPS, None, ALU.add).then_inc(var_ready, 1)
                dve.wait_ge(std_ready, n)
                link(nc.vector.reciprocal(rstd[:, :], rstd[:, :]))
                for t in range(T):
                    nc.vector.tensor_scalar(dst[:, t, :], src[:, t, :], mv[:, t, 0:1], rstd[:, t:t + 1],
                                            ALU.subtract, ALU.mult).then_inc(done, 1)

            layer_norm(xtm, xtm, 1, ln_done, x_loaded)
            dve.wait_ge(wv_made, 1)
            nc.vector.tensor_copy(wv[:, :, :], ps[:, 7, 0:KT * 2 * H].rearrange("p (k c) -> p k c", k=KT)).then_inc(wv_copied, 1)
            for t in range(T):
                dve.wait_ge(xw_done, t + 1)
                nc.vector.tensor_copy(ptm[:, t, :], ps[:, 4 + t % 3, 0:F])
                nc.vector.tensor_scalar(f2h[:, t * H:(t + 1) * H], ps[:, 4 + t % 3, F:F + H], 0.5, None, ALU.mult).then_inc(xw_copied, 1)

            def mask_steps(gp, t0, t1):
                with dve.Fori(t0, t1) as t:
                    for s in range(2):
                        dve.wait_ge(exp_done, t * 2 + (gp * T + s + 2))
                        if gp % 2 == 0:
                            dve.wait_ge(mask_loaded[s], (t + (gp // 2 * (T // 2) + 1)) * 16)
                        dve.wait_ge(e_free, gp * T + t * 2 + s + 1)
                        nc.vector.tensor_tensor(
                            buf_e[:, s, :].rearrange("p (h n) -> p h n", h=2),
                            buf_p[:, s, :].rearrange("p (h n) -> p h n", h=2),
                            mask[:, bass.ds(t * 2 + s, 1), :].to_broadcast([P, 2, HALF]),
                            ALU.mult).then_inc(masked, 1)

            def invert(gp):
                dve.wait_ge(den_moved, 32 * (gp + 1))
                link(nc.vector.tensor_scalar(den[:, :], den[:, :], TINY, None, ALU.max))
                nc.vector.reciprocal(den[:, :], den[:, :]).then_inc(inv_ready, 1)

            def normalise(gp):
                dve.wait_ge(inv_spread, 32 * (gp + 1))
                half, pair = gp % PASSES // 2, gp % 2
                for h in range(2):
                    q = slice(h * D, (h + 1) * D)
                    nc.vector.tensor_tensor(xc[q, pair, half * HALF:(half + 1) * HALF], raw[q, h, :], invb[q, :],
                                            ALU.mult).then_inc(xc_ready, 1)

            def attention(a):
                for q in range(PASSES):
                    gp = a * PASSES + q
                    if q:
                        mask_steps(gp, 0, 3)
                        invert(gp - 1)
                        mask_steps(gp, 3, 6)
                        normalise(gp - 1)
                        dve.wait_ge(xc_ready, 2 * gp)
                        mask_steps(gp, 6, T // 2)
                    else:
                        mask_steps(gp, 0, T // 2)
                    for b in range(2 * NB):
                        dve.wait_ge(bank_done, 2 * NB * gp + b + 1)
                        nc.vector.tensor_copy(raw[:, b // NB, b % NB * BLK:(b % NB + 1) * BLK], ps[:, b, 0:BLK]).then_inc(raw_copied, 1)
                invert(a * PASSES + PASSES - 1)
                normalise(a * PASSES + PASSES - 1)

            def batch_norm(n, src, g, b):
                for k in range(KT):
                    for c in range(BLOCKS):
                        hi = min((c + 1) * BLK, N)
                        last = nc.vector.bn_stats(bnst[:, k, c, :], src[:, k, c * BLK:hi])
                link(last)
                for k in range(KT):
                    last = nc.vector.bn_aggr(bnmv[:, k, :], bnst[:, k, :, :].rearrange("p a b -> p (a b)"))
                link(last)
                nc.vector.tensor_scalar(bnsc[:, :, 0], bnmv[:, :, 1], BN_EPS, None, ALU.add).then_inc(var_ready, 1)
                dve.wait_ge(std_ready, n)
                link(nc.vector.reciprocal(bnsc[:, :, 1], bnsc[:, :, 0]))
                link(nc.vector.tensor_tensor(bnsc[:, :, 2], bnsc[:, :, 1], vecs[:, g, :], ALU.mult))
                link(nc.vector.tensor_tensor(bnsc[:, :, 1], bnsc[:, :, 2], bnmv[:, :, 0], ALU.mult))
                link(nc.vector.tensor_tensor(bnsc[:, :, 3], vecs[:, b, :], bnsc[:, :, 1], ALU.subtract))
                for k in range(KT):
                    for c in range(2):
                        nc.vector.tensor_scalar(src[:, k, c * HALF:(c + 1) * HALF], src[:, k, c * HALF:(c + 1) * HALF],
                                                bnsc[:, k, 2:3], bnsc[:, k, 3:4], ALU.mult, ALU.add).then_inc(bn_applied, 1)

            def elu(base, dst, res):
                for u in range(UNITS):
                    m, b = u // BLOCKS, u % BLOCKS
                    cols = slice(b * BLK, (b + 1) * BLK)
                    dve.wait_ge(elu_relu, base + u + 1)
                    link(nc.vector.scalar_tensor_tensor(buf_p[:, m, cols], buf_s[:, m, cols], 1.0, buf_p[:, m, cols], ALU.min, ALU.add))
                    if res is None:
                        nc.vector.tensor_scalar(dst[:, m, cols], buf_p[:, m, cols], -1.0, None, ALU.add).then_inc(h_done, 1)
                    else:
                        nc.vector.scalar_tensor_tensor(dst[:, m, cols], buf_p[:, m, cols], -1.0, res[:, m, cols], ALU.add, ALU.add).then_inc(h_done, 1)

            attention(0)
            dve.wait_ge(xc_ready, 2 * PASSES)
            batch_norm(2, xc, ENC_G, ENC_B)
            elu(0, buf_e, xc)
            dve.wait_ge(h_done, UNITS)
            batch_norm(3, buf_e, EM_G, EM_B)
            attention(1)
            elu(UNITS, buf_e, None)
            elu(2 * UNITS, xc, buf_e)
            dve.wait_ge(h_done, 3 * UNITS)
            batch_norm(4, xc, DM_G, DM_B)
            dve.wait_ge(res_loaded, 16)
            for t in range(T):
                dve.wait_ge(ot_done, t + 1)
                last = nc.vector.tensor_tensor(x1[:, t, :], x1[:, t, :], ps[:, t % 8, 0:F], ALU.add).then_inc(x1_done, 1)
            dve.wait_ge(x1_done, T)
            layer_norm(x1, ptm, 5, ln2_done, None)
            dve.wait_ge(lg_done, 1)
            link(nc.vector.tensor_tensor(logits[:, :, :], ps[:, 7, 0:T * E].rearrange("p (t e) -> p t e", e=E),
                                         bg_sb[:, :].rearrange("p (a e) -> p a e", a=1).to_broadcast([P, T, E]), ALU.add))
            for t in range(T):
                last = nc.vector.max(top[:, t, :], logits[:, t, :])
            link(last)
            for t in range(T):
                last = nc.vector.max_index(topi[:, t, :], top[:, t, :], logits[:, t, :])
            link(last)
            nc.vector.tensor_copy(topf[:, :, :], topi[:, :, 0:2])
            nc.vector.tensor_tensor(gate[:, :, 0], top[:, :, 1], top[:, :, 0], ALU.subtract).then_inc(gate_in, 1)
            dve.wait_ge(gate_exp, 1)
            link(nc.vector.tensor_scalar(gate[:, :, 2], gate[:, :, 1], 1.0, None, ALU.add))
            link(nc.vector.reciprocal(gate[:, :, 2], gate[:, :, 2]))
            link(nc.vector.tensor_tensor(gate[:, :, 3], gate[:, :, 2], gate[:, :, 1], ALU.mult))
            for k in range(2):
                link(nc.vector.tensor_tensor(hot[:, k, :, :], eidx[:, :].rearrange("p (a e) -> p a e", a=1).to_broadcast([P, T, E]),
                                             topf[:, :, k:k + 1].to_broadcast([P, T, E]), ALU.is_equal))
                link(nc.vector.tensor_tensor(hot[:, k, :, :], hot[:, k, :, :], gate[:, :, 2 + k:3 + k].to_broadcast([P, T, E]), ALU.mult))
            link(nc.vector.tensor_tensor(comb[:, :, :], hot[:, 0, :, :], hot[:, 1, :, :], ALU.add))
            dve.sem_inc(comb_done, 1)
            for t in range(T):
                dve.wait_ge(ct_done, t + 1)
                nc.vector.tensor_copy(comb_t[:, (t % 2) * P:(t % 2 + 1) * P], ps[0:E, 4 + t % 2, 0:P]).then_inc(ct_copied, 1)
                dve.wait_ge(b2_done, t + 1)
                nc.vector.tensor_tensor(x1[:, t, :], x1[:, t, :], ps[:, 6, 0:F], ALU.add).then_inc(b2_added, 1)
            dve.wait_ge(b2_added, T)
            with dve.Fori(0, E) as e:
                with dve.Fori(0, FB) as n:
                    dve.wait_ge(down_done, e * FB + n + 2)
                    for i in range(TB):
                        row = x1[:, bass.ds(n * TB + i, 1), :].rearrange("p a f -> p (a f)")
                        last = nc.vector.scalar_tensor_tensor(
                            row, ps[:, 4 + i, 0:F],
                            comb[:, bass.ds(n * TB + i, 1), bass.ds(e, 1)].rearrange("p a f -> p (a f)"), row, ALU.mult, ALU.add)
                    last.then_inc(y_added, 1)

        @block.tensor
        def _(pe):
            pe.sem_inc(e_free, AHEAD)
            pe.sem_inc(down_done, 1)
            pe.wait_ge(ident_made, 2)
            pe.wait_ge(consts_loaded, ALL_CONSTS)
            for k in range(KT):
                last = nc.tensor.matmul(ps[:, 7, k * 2 * H:(k + 1) * 2 * H], wt_bd[:, k, :], v_bd[:, k, :], start=True, stop=True)
            last.then_inc(wv_made, 1)

            def transposes(src, ready, done, copied):
                for t in range(T):
                    pe.wait_ge(ready, t + 1)
                    if t >= 4:
                        pe.wait_ge(copied, t - 3)
                    for k in range(KT):
                        last = nc.tensor.transpose(ps[:, t % 4, k * P:(k + 1) * P], src[:, t, k * P:(k + 1) * P], ident[:, :])
                    last.then_inc(done, 1)

            transposes(xtm, ln_done, tr_done, tr_copied)
            pe.wait_ge(wv_copied, 1)
            for t in range(T):
                pe.wait_ge(tr_copied, t + 1)
                if t >= 3:
                    pe.wait_ge(xw_copied, t - 2)
                for k in range(KT):
                    nc.tensor.matmul(ps[:, 4 + t % 3, k * P:(k + 1) * P], buf_e[:, k, t * P:(t + 1) * P], w_bd[:, k, :], start=True, stop=True)
                for k in range(KT):
                    last = nc.tensor.matmul(ps[:, 4 + t % 3, F:F + H], buf_e[:, k, t * P:(t + 1) * P], wv[:, k, H:2 * H],
                                            start=(k == 0), stop=(k == KT - 1))
                last.then_inc(xw_done, 1)
            for b in range(BLOCKS):
                if b >= 4:
                    pe.wait_ge(f1_copied, b - 3)
                for k in range(KT):
                    last = nc.tensor.matmul(ps[0:H, b % 4, 0:BLK], wv[:, k, 0:H], buf_e[:, k, b * BLK:(b + 1) * BLK],
                                            start=(k == 0), stop=(k == KT - 1))
                last.then_inc(f1_done, 1)

            def product(gp, t, s, first, last_step):
                pe.wait_ge(masked, t * 2 + (gp * T + s + 1 + AHEAD))
                pe.wait_ge(stage_loaded[s], (t + (gp * (T // 2) + 1)) * 16)
                for h in range(2):
                    for b in range(NB):
                        if first and gp:
                            pe.wait_ge(raw_copied, 2 * NB * (gp - 1) + h * NB + b + 1)
                        mm = nc.tensor.matmul(ps[:, h * NB + b, 0:BLK], stage[:, s, h * D:h * D + P],
                                              buf_e[:, s, h * HALF + b * BLK:h * HALF + (b + 1) * BLK],
                                              start=first, stop=last_step)
                        if last_step:
                            mm.then_inc(bank_done, 1)
                if last_step:
                    pe.wait_ge(bank_done, 2 * NB * (gp + 1))
                    pe.sem_inc(e_free, 1)
                else:
                    mm.then_inc(e_free, 1)

            def attention(a):
                for q in range(PASSES):
                    gp = a * PASSES + q
                    product(gp, 0, 0, True, False)
                    product(gp, 0, 1, False, False)
                    with pe.Fori(1, T // 2 - 1) as t:
                        product(gp, t, 0, False, False)
                        product(gp, t, 1, False, False)
                    product(gp, T // 2 - 1, 0, False, False)
                    product(gp, T // 2 - 1, 1, False, True)

            def layer(base, wsb, src, ready, count):
                for u in range(UNITS):
                    m, b = u // BLOCKS, u % BLOCKS
                    if u == 0:
                        pe.wait_ge(ready, count)
                    if u >= 8:
                        pe.wait_ge(elu_relu, base + u - 7)
                    if wsb is wt_bd:
                        mm = nc.tensor.matmul(ps[:, u % 8, 0:BLK], wt_bd_use[:, m, :], src[:, m, b * BLK:(b + 1) * BLK], start=True, stop=True)
                    else:
                        for k in range(KT):
                            mm = nc.tensor.matmul(ps[:, u % 8, 0:BLK], wsb[:, k, m * P:(m + 1) * P], src[:, k, b * BLK:(b + 1) * BLK],
                                                  start=(k == 0), stop=(k == KT - 1))
                    mm.then_inc(z_done, 1)

            wt_bd_use = wt_bd
            attention(0)
            pe.wait_ge(raw_copied, 2 * NB * PASSES)
            layer(0, emw_sb, xc, bn_applied, 4)
            pe.wait_ge(bn_applied, 8)
            for t in range(T // 2):
                if t < 8:
                    pe.wait_ge(elu_relu, UNITS)
                else:
                    pe.wait_ge(et_copied, t - 7)
                for i in range(2):
                    for k in range(KT):
                        last = nc.tensor.transpose(ps[:, t % 8, i * F + k * P:i * F + (k + 1) * P],
                                                   buf_e[:, k, (2 * t + i) * P:(2 * t + i + 1) * P], ident[:, :])
                last.then_inc(et_done, 1)
            pe.wait_ge(et_copied, T // 2)
            attention(1)
            pe.wait_ge(raw_copied, 4 * NB * PASSES)
            layer(UNITS, wt_bd, xc, xc_ready, 4 * PASSES)
            pe.wait_ge(elu_relu, 2 * UNITS)
            layer(2 * UNITS, dmw_sb, buf_e, h_done, 2 * UNITS)
            pe.wait_ge(elu_relu, 3 * UNITS)
            pe.wait_ge(bn_applied, 12)
            for t in range(T):
                if t >= 8:
                    pe.wait_ge(x1_done, t - 7)
                for k in range(KT):
                    last = nc.tensor.transpose(ps[:, t % 8, k * P:(k + 1) * P], xc[:, k, t * P:(t + 1) * P], ident[:, :])
                last.then_inc(ot_done, 1)
            pe.wait_ge(x1_done, T)
            transposes(ptm, ln2_done, tr2_done, tr2_copied)
            pe.wait_ge(tr2_copied, T)
            for t in range(T):
                for k in range(KT):
                    last = nc.tensor.matmul(ps[:, 7, t * E:(t + 1) * E], buf_e[:, k, t * P:(t + 1) * P], wg_sb[:, k, :],
                                            start=(k == 0), stop=(k == KT - 1))
            last.then_inc(lg_done, 1)
            pe.wait_ge(comb_done, 1)
            for t in range(T):
                if t >= 2:
                    pe.wait_ge(ct_copied, t - 1)
                nc.tensor.transpose(ps[0:E, 4 + t % 2, 0:P], comb[:, t, :], ident[:, :]).then_inc(ct_done, 1)
                pe.wait_ge(ct_copied, t + 1)
                if t:
                    pe.wait_ge(b2_added, t)
                nc.tensor.matmul(ps[:, 6, 0:F], comb_t[:, (t % 2) * P:(t % 2 + 1) * P], b2_sb[:, :], start=True, stop=True).then_inc(b2_done, 1)
            pe.wait_ge(b2_added, T)
            with pe.Fori(0, E // 2) as e2:
                for s in range(2):
                    with pe.Fori(0, FB) as n:
                        pe.wait_ge(w_loaded[s], (e2 + 1) * 32)
                        for f in range(FT):
                            for k in range(KT):
                                mm = nc.tensor.matmul(ps[:, f // 2, (f % 2) * 256:(f % 2) * 256 + 256], w1_sb[:, s, k, f * P:(f + 1) * P],
                                                      buf_e[:, k, bass.ds(n * (TB * P), TB * P)], start=(k == 0), stop=(k == KT - 1))
                            mm.then_inc(up_done, 1)
                        pe.wait_ge(relu_done, e2 * (2 * FB * FT) + n * FT + (s * FB * FT + FT))
                        pe.wait_ge(y_added, e2 * (2 * FB) + n + (s * FB + 1))
                        for i in range(TB):
                            for f in range(FT):
                                mm = nc.tensor.matmul(ps[:, 4 + i, 0:F], h_sb[:, f, i * P:(i + 1) * P], w2_sb[:, s, f, :],
                                                      start=(f == 0), stop=(f == FT - 1))
                        mm.then_inc(down_done, 1)


_OUT = ("out_dram", (N, F))


def kernel(x, adj, L0_gnn_W, L0_gnn_V, L0_gnn_enc_bn_gamma, L0_gnn_enc_bn_beta, L0_gnn_enc_mlp_W, L0_gnn_enc_mlp_b,
           L0_gnn_enc_mlp_bn_gamma, L0_gnn_enc_mlp_bn_beta, L0_gnn_dec_mlp_W, L0_gnn_dec_mlp_b,
           L0_gnn_dec_mlp_bn_gamma, L0_gnn_dec_mlp_bn_beta, L0_ffn_Wg, L0_ffn_bg, L0_ffn_W1, L0_ffn_b1,
           L0_ffn_W2, L0_ffn_b2):
    import numpy as np
    import concourse.bacc as bacc
    from concourse.bass_utils import run_bass_kernel_spmd

    xp = np.zeros((NP, F), np.float32)
    xp[:N] = np.asarray(x)
    adj_t = np.zeros((NP, NP), np.float32)
    adj_t[:N, :N] = np.asarray(adj).T
    w = np.asarray(L0_gnn_W)
    host = {
        "x": xp, "adj_t": adj_t, "w": w, "wt": w.transpose(0, 2, 1), "v": L0_gnn_V,
        "enc_g": L0_gnn_enc_bn_gamma, "enc_b": L0_gnn_enc_bn_beta,
        "emw_t": np.asarray(L0_gnn_enc_mlp_W).T, "emb": L0_gnn_enc_mlp_b,
        "em_g": L0_gnn_enc_mlp_bn_gamma, "em_b": L0_gnn_enc_mlp_bn_beta,
        "dmw_t": np.asarray(L0_gnn_dec_mlp_W).T, "dmb": L0_gnn_dec_mlp_b,
        "dm_g": L0_gnn_dec_mlp_bn_gamma, "dm_b": L0_gnn_dec_mlp_bn_beta,
        "wg": L0_ffn_Wg, "bg": L0_ffn_bg, "w1": L0_ffn_W1, "b1": L0_ffn_b1, "w2": L0_ffn_W2, "b2": L0_ffn_b2,
    }
    nc = bacc.Bacc("TRN2", target_bir_lowering=False, num_devices=1)
    arrays, args = {}, {}
    for name, a in host.items():
        a = np.ascontiguousarray(np.asarray(a))
        arrays[f"in_{name}"] = a
        args[name] = nc.dram_tensor(f"in_{name}", a.shape, mybir.dt.from_np(a.dtype), kind="ExternalInput").ap()
    out = nc.dram_tensor(_OUT[0], _OUT[1], F32, kind="ExternalOutput").ap()
    build(nc, out=out, **args)
    r = run_bass_kernel_spmd(nc, [arrays], core_ids=[0])
    return r.results[0][_OUT[0]]
```

```python
from contextlib import ExitStack

import concourse.bass as bass
from concourse import mybir

F32 = mybir.dt.float32
U8 = mybir.dt.uint8
U32 = mybir.dt.uint32
I32 = mybir.dt.int32
F16 = mybir.dt.float16
ALU = mybir.AluOpType
ACT = mybir.ActivationFunctionType

P = 128
N = 3327
T = -(-N // P)
NP = T * P
F = 256
KT = F // P
H = 4
D = F // H
HALF = NP // 2
NB = 4
BLK = HALF // NB
BLOCKS = 2 * NB
PASSES = 4
E = 8
FF = 1024
FT = FF // P
PAIRS = 2 * T
S = PAIRS + E
GRAN = 512
WG = KT * FF // GRAN
W_SCALE = 64.0
X_SCALE = 4.0
H_SCALE = W_SCALE * X_SCALE
Y_SCALE = H_SCALE * W_SCALE
LN_EPS = 1e-5
BN_EPS = 1e-6
TINY = 1e-30
AHEAD = 2


def build(nc, x, adj_t, w, wt, v, enc_g, enc_b, emw_t, emb, em_g, em_b, dmw_t, dmb, dm_g, dm_b,
          wg, bg, w1, b1, w2, b2, out):
    xw_dram = nc.dram_tensor("xw_scratch", [NP, F], F32, kind="Internal").ap()
    f1_dram = nc.dram_tensor("f1_scratch", [H, NP], F32, kind="Internal").ap()
    xs_dram = nc.dram_tensor("expert_input_scratch", [S * P, F], F32, kind="Internal").ap()
    ys_dram = nc.dram_tensor("expert_output_scratch", [S * P, F], F32, kind="Internal").ap()
    inv_dram = nc.dram_tensor("inv_scratch", [2 * PASSES, 2, HALF], F32, kind="Internal").ap()

    with ExitStack() as ctx:
        def sb(name, shape, dt=F32, scope=ctx):
            return scope.enter_context(nc.sbuf_tensor(name, shape, dt))

        def sem(name):
            return ctx.enter_context(nc.semaphore(name))

        ident = sb("ident", [P, P])
        w_bd = sb("w_bd", [P, KT, P])
        wt_bd = sb("wt_bd", [P, KT, P])
        v_bd = sb("v_bd", [P, KT, 2 * H])
        wv = sb("wv", [P, KT, 2 * H])
        emw_sb = sb("emw_sb", [P, KT, F])
        dmw_sb = sb("dmw_sb", [P, KT, F])
        vecs = sb("vecs", [P, 8, KT])
        ENC_G, ENC_B, EMB, EM_G, EM_B, DMB, DM_G, DM_B = range(8)
        bg_sb = sb("bg_sb", [P, E])
        wg_sb = sb("wg_sb", [P, KT, E])
        b1_sb = sb("b1_sb", [P, E, FT])
        b2_sb = sb("b2_sb", [E, F])
        f2h = sb("f2h", [P, T * H])
        stats = sb("stats", [P, T, 6])
        mv = sb("mv", [P, T, 2])
        rstd = sb("rstd", [P, T])
        bnst = sb("bnst", [P, KT, BLOCKS, 6])
        bnmv = sb("bnmv", [P, KT, 2])
        bnsc = sb("bnsc", [P, KT, 4])
        den = sb("den", [P, 2 * HALF // P])
        b1s = sb("b1s", [P, E, FT])

        stage = sb("stage", [P, 2, 3 * D])

        with ExitStack() as later:
            x1 = sb("x1", [P, T, F], F32, later)
            w1p = sb("w1p", [P, E * WG + 1, 2 * GRAN], F16, later)
        mask = sb("mask", [P, T, HALF], U8)
        f1b = sb("f1b", [P, 2, 2, HALF])
        raw = sb("raw", [P, 2, HALF])
        invb = sb("invb", [P, HALF])
        sb("pad", [P, (T * F * 4 + (E * WG + 1) * GRAN * 4 - T * HALF - 7 * HALF * 4) // 4])
        with ExitStack() as later:
            xt = sb("xt", [P, 2, F], F32, later)
            xtp = sb("xtp", [P, 2, 2, KT, P], F16, later)
            hb = sb("hb", [P, 2, FT * P], F32, later)
            hp = sb("hp", [P, 2, 2, FT, P], F16, later)
            ysb = sb("ysb", [P, 2, F], F32, later)
            got = sb("got", [P, 4, F], F32, later)
            w2p = sb("w2p", [P, E * WG + 1, 2 * GRAN], F16, later)
            logits = sb("logits", [P, T, E], F32, later)
            top = sb("top", [P, T, 8], F32, later)
            topi = sb("topi", [P, T, 8], U32, later)
            topf = sb("topf", [P, T, 2], F32, later)
            count_u = sb("count_u", [P, S], U32, later)
            count = sb("count", [P, S], F32, later)
            gate = sb("gate", [P, T, 4], F32, later)
            hot = sb("hot", [P, 2, T, E], F32, later)
            comb = sb("comb", [P, T, E], F32, later)
            both = sb("both", [P, T, E], F32, later)
            pre = sb("pre", [P, 2, T, E], F32, later)
            ends = sb("ends", [P, 6, E], F32, later)
            slot = sb("slot", [P, 2, T], F32, later)
            slot_u = sb("slot_u", [P, 2, T], U32, later)
            eid = sb("eid", [P, S], I32, later)
            before = sb("before", [P, P], F32, later)
            ones = sb("ones", [P, P], F32, later)
            comb_t = sb("comb_t", [E, P * 2], F32, later)
        buf_p = sb("buf_p", [P, 2, NP])
        buf_e = sb("buf_e", [P, 2, NP])
        buf_s = sb("buf_s", [P, 2, NP])
        xc = sb("xc", [P, KT, NP])

        ps = ctx.enter_context(nc.psum_tensor("ps", [P, 8, 512], F32))

        x_loaded = [sem(f"x_loaded{i}") for i in range(2)]
        consts_loaded = sem("consts_loaded")
        zeroed = sem("zeroed")
        ident_made = sem("ident_made")
        wv_made = sem("wv_made")
        wv_copied = sem("wv_copied")
        dve_step = sem("dve_step")
        var_ready = sem("var_ready")
        std_ready = sem("std_ready")
        ln_done = sem("ln_done")
        tr_done = sem("tr_done")
        tr_copied = sem("tr_copied")
        xw_done = sem("xw_done")
        xw_copied = sem("xw_copied")
        f1_done = sem("f1_done")
        f1_copied = sem("f1_copied")
        f1_stored = sem("f1_stored")
        xw_stored = sem("xw_stored")
        f1b_loaded = [sem(f"f1b_loaded{i}") for i in range(2)]
        stage_loaded = [sem(f"stage_loaded{i}") for i in range(2)]
        mask_loaded = [sem(f"mask_loaded{i}") for i in range(2)]
        tanh_done = sem("tanh_done")
        exp_done = sem("exp_done")
        masked = sem("masked")
        multiplied = sem("multiplied")
        e_free = sem("e_free")
        bank_done = sem("bank_done")
        raw_copied = sem("raw_copied")
        den_moved = sem("den_moved")
        inv_ready = sem("inv_ready")
        inv_stored = sem("inv_stored")
        inv_spread = sem("inv_spread")
        xc_ready = sem("xc_ready")
        bn_applied = sem("bn_applied")
        z_done = sem("z_done")
        elu_exp = sem("elu_exp")
        elu_relu = sem("elu_relu")
        h_done = sem("h_done")
        emb_done = sem("emb_done")
        et_done = sem("et_done")
        et_copied = sem("et_copied")
        emb_stored = sem("emb_stored")
        res_loaded = sem("res_loaded")
        ot_done = sem("ot_done")
        x1_done = sem("x1_done")
        ln2_done = sem("ln2_done")
        tr2_done = sem("tr2_done")
        tr2_copied = sem("tr2_copied")
        lg_done = sem("lg_done")
        gate_exp = sem("gate_exp")
        gate_in = sem("gate_in")
        comb_done = sem("comb_done")
        ct_done = sem("ct_done")
        ct_copied = sem("ct_copied")
        b2_done = sem("b2_done")
        b2_added = sem("b2_added")
        small_free = sem("small_free")
        tri_made = sem("tri_made")
        hot_ready = sem("hot_ready")
        pos_done = sem("pos_done")
        slots_ready = sem("slots_ready")
        filled = sem("filled")
        scattered = sem("scattered")
        w1_staged = [sem(f"w1_staged{e}") for e in range(E)]
        w2_staged = [sem(f"w2_staged{e}") for e in range(E)]
        w_high = sem("w_high")
        w_low = sem("w_low")
        b1_scaled = sem("b1_scaled")
        xt_loaded = [sem(f"xt_loaded{i}") for i in range(2)]
        xt_transposed = sem("xt_transposed")
        x_high = sem("x_high")
        x_low = sem("x_low")
        up_done = sem("up_done")
        biased = sem("biased")
        h_high = sem("h_high")
        h_low = sem("h_low")
        down_done = sem("down_done")
        y_copied = sem("y_copied")
        ys_stored = [sem(f"ys_stored{i}") for i in range(2)]
        gathered = [sem(f"gathered{i}") for i in range(4)]
        combined = sem("combined")
        out_stored = sem("out_stored")

        def wait(eng, semaphore, value):
            if not isinstance(value, int) or value > 0:
                eng.wait_ge(semaphore, value)

        def tiles_in_flight(eng, step):
            step(0, 0)
            step(1, 1)
            with eng.Fori(1, S // 2 - 1) as n:
                step(n * 2, 0)
                step(n * 2 + 1, 1)
            step(S - 2, 0)
            step(S - 1, 1)

        def half_count(i, s, more=0):
            return i // 2 + more if isinstance(i, int) else (i - s) // 2 + more

        xtm = buf_s[:, :, :].rearrange("p a n -> p (a n)").rearrange("p (t f) -> p t f", f=F)
        ptm = buf_p[:, :, :].rearrange("p a n -> p (a n)").rearrange("p (t f) -> p t f", f=F)
        f1row = raw[0:H, :, :].rearrange("p a n -> p (a n)")
        x_tm = x.rearrange("(t p) f -> p t f", p=P)
        T0 = T // 2

        consts = []
        for h in range(H):
            q = slice((h % 2) * D, (h % 2) * D + D)
            consts.append((w_bd[q, h // 2, q], w[h]))
            consts.append((wt_bd[q, h // 2, q], wt[h]))
            for k in range(2):
                consts.append((v_bd[q, h // 2, H * k + h:H * k + h + 1], v[h, k]))
        for n, a in enumerate((enc_g, enc_b, emb, em_g, em_b, dmb, dm_g, dm_b)):
            consts.append((vecs[:, n, :], a.rearrange("(t p) -> p t", p=P)))
        consts += [(emw_sb[:, :, :], emw_t.rearrange("(t p) o -> p t o", p=P)),
                   (dmw_sb[:, :, :], dmw_t.rearrange("(t p) o -> p t o", p=P)),
                   (wg_sb[:, :, :], wg.rearrange("(t p) e -> p t e", p=P)),
                   (b1_sb[:, :, :], b1.rearrange("e (t p) -> p e t", p=P)),
                   (b2_sb[:, :], b2),
                   (bg_sb[:, :], bg.rearrange("(a e) -> a e", a=1).to_broadcast([P, E]))]
        ALL_CONSTS = 16 * len(consts)
        STEPS = T * PASSES
        UNITS = KT * BLOCKS

        def splits():
            n = 0
            for g in range(E * WG):
                for w_sb, gg in ((w1p, g), (w2p, E * WG - 1 - g)):
                    src = w_sb[:, gg + 1 if w_sb is w1p else gg, :].bitcast(F32)
                    yield w_sb, gg, src, n
                    n += 1

        def w_sb_staged(w_sb, g):
            return (w1_staged if w_sb is w1p else w2_staged)[g // WG]

        block = ctx.enter_context(nc.Block())

        @block.sync
        def _(sp):
            for i in range(2):
                sp.dma_start(xtm[:, i * T0:(i + 1) * T0, :], x_tm[:, i * T0:(i + 1) * T0, :]).then_inc(x_loaded[i], 16)
            sp.wait_ge(zeroed, 3)
            with nc.allow_non_contiguous_dma(reason="small vectors"):
                for dst, src in consts:
                    sp.dma_start(dst, src).then_inc(consts_loaded, 16)
            sp.wait_ge(xw_copied, T)
            sp.dma_start(xw_dram.rearrange("(t p) f -> p t f", p=P), ptm).then_inc(xw_stored, 16)
            sp.wait_ge(f1_copied, BLOCKS)
            sp.dma_start(f1_dram, f1row).then_inc(f1_stored, 16)

            def load_f1(gp):
                half, pair = gp % PASSES // 2, gp % 2
                if gp >= 2:
                    sp.wait_ge(tanh_done, 2 * T * (gp - 1))
                src = f1_dram[2 * pair:2 * pair + 2, half * HALF:(half + 1) * HALF]
                sp.dma_start(f1b[:, gp % 2, :, :], src.rearrange("(a h) n -> a h n", a=1).to_broadcast([P, 2, HALF])) \
                    .then_inc(f1b_loaded[gp % 2], 16)

            sp.wait_ge(f1_stored, 16)
            load_f1(0)
            sp.wait_ge(xw_stored, 16)
            for gp in range(2 * PASSES):
                pair = gp % 2
                if gp + 1 < 2 * PASSES:
                    load_f1(gp + 1)
                if gp == PASSES:
                    sp.wait_ge(emb_stored, 16)
                with sp.Fori(0, T // 2) as t:
                    for s in range(2):
                        sp.wait_ge(e_free, gp * T + t * 2 + s + 1)
                        sp.dma_start(
                            stage[:, s, :].rearrange("p (c d) -> p c d", d=D)[:, 0:3:2, :],
                            xw_dram[bass.ds(t * (2 * P) + s * P, P), pair * P:(pair + 1) * P]
                            .rearrange("p (c d) -> p c d", d=D)).then_inc(stage_loaded[s], 16)
                if gp == PASSES - 1:
                    sp.wait_ge(et_copied, T // 2)
                    sp.dma_start(xw_dram.rearrange("(t p) f -> p t f", p=P), xtm).then_inc(emb_stored, 16)
            sp.wait_ge(masked, 2 * STEPS + AHEAD)
            sp.wait_ge(xc_ready, 4 * PASSES)
            sp.dma_start(x1[:, :, :], x_tm).then_inc(res_loaded, 16)
            for e in range(E):
                dst = w1p[:, e * WG + 1:(e + 1) * WG + 1, :].rearrange("p g c -> p (g c)").bitcast(F32)
                sp.dma_start(dst.rearrange("p (k f) -> p k f", k=KT), w1[e].rearrange("(k p) f -> p k f", p=P)).then_inc(w1_staged[e], 16)
            for e in reversed(range(E)):
                if e == E - 1:
                    sp.wait_ge(h_done, 3 * UNITS)
                    sp.wait_ge(x1_done, T)
                if e == 3:
                    sp.wait_ge(lg_done, 1)
                dst = w2p[:, e * WG:(e + 1) * WG, :].rearrange("p g c -> p (g c)").bitcast(F32)
                sp.dma_start(dst.rearrange("p (t f) -> p t f", t=FT), w2[e].rearrange("(t p) f -> p t f", p=P)).then_inc(w2_staged[e], 16)
            sp.wait_ge(scattered, 16 * PAIRS)

            def load_x(i, s):
                wait(sp, xt_transposed, i - 1)
                sp.dma_start(xt[:, s, :], xs_dram[bass.ds(i * P, P), :]).then_inc(xt_loaded[s], 16)

            def step(i, s):
                if not (isinstance(i, int) and i + 2 >= S):
                    load_x(i + 2, s)
                sp.wait_ge(y_copied, i + 1)
                sp.dma_start(ys_dram[bass.ds(i * P, P), :], ysb[:, s, :]).then_inc(ys_stored[s], 16)

            load_x(0, 0)
            load_x(1, 1)
            tiles_in_flight(sp, step)
            for t in range(T):
                rows = min(P, N - t * P)
                sp.wait_ge(combined, 2 * (t + 1))
                sp.dma_start(out[t * P:t * P + rows, :], x1[0:rows, t, :]).then_inc(out_stored, 16)
            sp.wait_ge(out_stored, 16 * T)

        @block.gpsimd
        def _(pool):
            nc.gpsimd.memset(w_bd[:, :, :], 0.0).then_inc(zeroed, 1)
            nc.gpsimd.memset(wt_bd[:, :, :], 0.0).then_inc(zeroed, 1)
            nc.gpsimd.memset(v_bd[:, :, :], 0.0).then_inc(zeroed, 1)
            nc.gpsimd.memset(ident[:, :], 0.0).then_inc(zeroed, 1)
            nc.gpsimd.memset(stage[:, :, :], 1.0).then_inc(zeroed, 1)
            nc.gpsimd.memset(xc[:, :, :], 0.0).then_inc(zeroed, 1)
            pool.wait_ge(zeroed, 6)
            nc.gpsimd.affine_select(out=ident[:, :], in_=ident[:, :], compare_op=ALU.not_equal, fill=1.0,
                                    base=0, pattern=[[-1, P]], channel_multiplier=1).then_inc(ident_made, 1)
            fill = xs_dram.rearrange("(p s) f -> p (s f)", p=P)
            for c in range(0, S, T):
                n = min(T, S - c) * F
                pool.dma_start(fill[:, c * F:c * F + n], xc[:, :, :].rearrange("p k n -> p (k n)")[:, 0:n],
                               max_dma_last_dim=16384).then_inc(filled, 16)

            def load_masks(count, half, after):
                def load_pair(t):
                    for s in range(2):
                        if after is not None:
                            pool.wait_ge(masked, t * 2 + (after + s + 1 + AHEAD))
                        if count or not isinstance(t, int):
                            pool.wait_ge(mask_loaded[s], (t + count * (T // 2)) * 16)
                        pool.dma_start(mask[:, bass.ds(t * 2 + s, 1), :].rearrange("p a n -> p (a n)"),
                                       adj_t[bass.ds(t * (2 * P) + s * P, P), half * HALF:(half + 1) * HALF]) \
                            .then_inc(mask_loaded[s], 16)

                load_pair(0)
                with pool.Fori(1, T // 2) as t:
                    load_pair(t)

            def spread_inverse(gp):
                pool.wait_ge(raw_copied, 2 * NB * (gp + 1))
                for h in range(2):
                    row = D * (1 - h)
                    pool.dma_start(den[:, h * (HALF // P):(h + 1) * (HALF // P)],
                                   raw[row:row + 1, h, :]).then_inc(den_moved, 16)
                pool.wait_ge(inv_ready, gp + 1)
                for h in range(2):
                    pool.dma_start(inv_dram[gp, h].rearrange("(p c) -> p c", p=P),
                                   den[:, h * (HALF // P):(h + 1) * (HALF // P)]).then_inc(inv_stored, 16)
                pool.wait_ge(inv_stored, 32 * (gp + 1))
                for h in range(2):
                    pool.dma_start(invb[h * D:(h + 1) * D, :],
                                   inv_dram[gp, h:h + 1].to_broadcast([D, HALF])).then_inc(inv_spread, 16)

            load_masks(0, 0, None)
            for gp in range(2 * PASSES):
                if gp:
                    spread_inverse(gp - 1)
                if gp % 2 and gp + 1 < 2 * PASSES:
                    load_masks((gp + 1) // 2, (gp // 2 + 1) % 2, gp * T)
            spread_inverse(2 * PASSES - 1)

            pool.wait_ge(x1_done, T)
            nc.gpsimd.iota(count_u[:, :], [[1, S]], base=0, channel_multiplier=0).then_inc(small_free, 1)
            nc.gpsimd.memset(ones[:, :], 1.0).then_inc(small_free, 1)
            pool.wait_ge(small_free, 2)
            nc.gpsimd.tensor_copy(count[:, :], count_u[:, :]).then_inc(tri_made, 1)
            nc.gpsimd.affine_select(out=before[:, :], in_=ones[:, :], compare_op=ALU.is_gt, fill=0.0,
                                    base=0, pattern=[[1, P]], channel_multiplier=-1).then_inc(tri_made, 1)
            pool.wait_ge(slots_ready, 1)
            pool.wait_ge(ln2_done, T)
            for t in range(T):
                for k in range(2):
                    nc.gpsimd.indirect_dma_start(
                        out=xs_dram, out_offset=bass.IndirectOffsetOnAxis(ap=slot_u[:, k, t:t + 1], axis=0),
                        in_=ptm[:, t, :], in_offset=None, bounds_check=S * P - 1, oob_is_err=False).then_inc(scattered, 16)
            for s in range(2):
                pool.wait_ge(ys_stored[s], 16 * (S // 2))
            for t in range(T):
                for k in range(2):
                    n = 2 * t + k
                    if n >= 4:
                        pool.wait_ge(combined, n - 3)
                    nc.gpsimd.indirect_dma_start(
                        out=got[:, n % 4, :], out_offset=None,
                        in_=ys_dram, in_offset=bass.IndirectOffsetOnAxis(ap=slot_u[:, k, t:t + 1], axis=0),
                        bounds_check=S * P - 1, oob_is_err=False).then_inc(gathered[n % 4], 16)

        @block.scalar
        def _(act):
            act.sem_inc(exp_done, 1)
            act.wait_ge(var_ready, 1)
            nc.scalar.activation(rstd[:, :], rstd[:, :], ACT.Sqrt).then_inc(std_ready, 1)

            def copy_transposed(t, done, copied, dst):
                act.wait_ge(done, t + 1)
                nc.scalar.activation(dst[:, :, t * P:(t + 1) * P],
                                     ps[:, t % 4, 0:F].rearrange("p (k n) -> p k n", k=KT), ACT.Copy).then_inc(copied, 1)

            for t in range(T):
                copy_transposed(t, tr_done, tr_copied, buf_e)
            for b in range(BLOCKS):
                act.wait_ge(f1_done, b + 1)
                nc.scalar.activation(f1row[:, b * BLK:(b + 1) * BLK], ps[0:H, b % 4, 0:BLK], ACT.Copy).then_inc(f1_copied, 1)

            def tanh(gp, jt, s):
                act.wait_ge(exp_done, jt + gp * T if gp or not isinstance(jt, int) else max(jt, 1))
                for h in range(2):
                    col = jt * H + (gp % 2) * 2 + h
                    nc.scalar.activation(buf_s[:, s, h * HALF:(h + 1) * HALF], f1b[:, gp % 2, h, :], ACT.Tanh,
                                         bias=f2h[:, bass.ds(col, 1)], scale=0.5).then_inc(tanh_done, 1)

            def exp(step, s):
                act.wait_ge(tanh_done, step * 2 + 2)
                act.wait_ge(masked, step + 1)
                nc.scalar.activation(buf_p[:, s, :], buf_s[:, s, :], ACT.Exp, scale=0.5).then_inc(exp_done, 1)

            def attention(a):
                for q in range(PASSES):
                    gp = a * PASSES + q
                    g0 = gp * T
                    act.wait_ge(f1b_loaded[gp % 2], 16 * (gp // 2 + 1))
                    tanh(gp, 0, 0)
                    with act.Fori(0, T // 2 - 1) as t:
                        tanh(gp, t * 2 + 1, 1)
                        exp(t * 2 + g0, 0)
                        tanh(gp, t * 2 + 2, 0)
                        exp(t * 2 + (g0 + 1), 1)
                    tanh(gp, T - 1, 1)
                    exp(g0 + T - 2, 0)
                    exp(g0 + T - 1, 1)

            def bn_sqrt(n):
                act.wait_ge(var_ready, n + 1)
                nc.scalar.activation(bnsc[:, :, 0], bnsc[:, :, 0], ACT.Sqrt).then_inc(std_ready, 1)

            def elu_parts(base, bias):
                for u in range(UNITS):
                    m, b = u // BLOCKS, u % BLOCKS
                    cols = slice(b * BLK, (b + 1) * BLK)
                    act.wait_ge(z_done, base + u + 1)
                    z = ps[:, u % 8, 0:BLK]
                    bb = 0.0 if bias is None else vecs[:, bias, m:m + 1]
                    nc.scalar.activation(buf_s[:, m, cols], z, ACT.Exp, bias=bb).then_inc(elu_exp, 1)
                    nc.scalar.activation(buf_p[:, m, cols], z, ACT.Relu, bias=bb).then_inc(elu_relu, 1)

            act.wait_ge(xw_copied, T)
            act.wait_ge(xw_stored, 16)
            attention(0)
            bn_sqrt(1)
            elu_parts(0, EMB)
            bn_sqrt(2)
            for t in range(T // 2):
                act.wait_ge(et_done, t + 1)
                nc.scalar.activation(xtm[:, 2 * t:2 * t + 2, :], ps[:, t % 8, :].rearrange("p (t f) -> p t f", f=F),
                                     ACT.Copy).then_inc(et_copied, 1)
            act.wait_ge(emb_stored, 16)
            attention(1)
            elu_parts(UNITS, None)
            elu_parts(2 * UNITS, DMB)
            bn_sqrt(3)
            act.wait_ge(var_ready, 5)
            nc.scalar.activation(rstd[:, :], rstd[:, :], ACT.Sqrt).then_inc(std_ready, 1)
            for t in range(T):
                copy_transposed(t, tr2_done, tr2_copied, buf_e)
            act.wait_ge(gate_in, 1)
            nc.scalar.activation(gate[:, :, 1], gate[:, :, 0], ACT.Exp).then_inc(gate_exp, 1)
            for w_sb, g, src, n in splits():
                act.wait_ge(w_sb_staged(w_sb, g), 16)
                if n >= 2:
                    act.wait_ge(w_low, n - 1)
                nc.scalar.activation(w_sb[:, g, 0:GRAN] if w_sb is w1p else w_sb[:, g + 1, 0:GRAN],
                                     src, ACT.Copy, scale=W_SCALE).then_inc(w_high, 1)

            def x_half(i, s):
                act.wait_ge(xt_transposed, i + 1)
                wait(act, up_done, i - 1)
                nc.scalar.activation(xtp[:, s, 0, :, :], ps[:, 6 + s, 0:F].rearrange("p (k n) -> p k n", k=KT), ACT.Copy,
                                     scale=X_SCALE).then_inc(x_high, 1)

            def h_half(i, s):
                act.wait_ge(biased, i + 1)
                wait(act, down_done, i - 1)
                nc.scalar.activation(hp[:, s, 0, :, :], hb[:, s, :].rearrange("p (f n) -> p f n", f=FT), ACT.Relu).then_inc(h_high, 1)

            def step(i, s):
                last = isinstance(i, int) and i + 2 >= S
                if not last:
                    x_half(i + 2, s)
                if not last or i + 1 < S:
                    h_half(i + 1, 1 - s)
                act.wait_ge(down_done, i + 1)
                if not isinstance(i, int) or i >= 2:
                    act.wait_ge(ys_stored[s], half_count(i, s) * 16)
                nc.scalar.activation(ysb[:, s, :], ps[:, 4 + s, 0:F], ACT.Copy, scale=1.0 / Y_SCALE).then_inc(y_copied, 1)

            act.wait_ge(scattered, 16 * PAIRS)
            x_half(0, 0)
            x_half(1, 1)
            h_half(0, 0)
            tiles_in_flight(act, step)

        @block.vector
        def _(dve):
            steps = [0]

            def link(ins):
                steps[0] += 1
                ins.then_inc(dve_step, 1)
                dve.wait_ge(dve_step, steps[0])

            dve.sem_inc(masked, AHEAD)
            dve.wait_ge(consts_loaded, ALL_CONSTS)
            dve.wait_ge(ident_made, 1)

            def layer_norm(src, dst, n, done, loaded):
                for t in range(T):
                    if loaded is not None and t % T0 == 0:
                        dve.wait_ge(loaded[t // T0], 16)
                    last = nc.vector.bn_stats(stats[:, t, :], src[:, t, :])
                link(last)
                for t in range(T):
                    last = nc.vector.bn_aggr(mv[:, t, :], stats[:, t, :])
                link(last)
                nc.vector.tensor_scalar(rstd[:, :], mv[:, :, 1], LN_EPS, None, ALU.add).then_inc(var_ready, 1)
                dve.wait_ge(std_ready, n)
                link(nc.vector.reciprocal(rstd[:, :], rstd[:, :]))
                for t in range(T):
                    nc.vector.tensor_scalar(dst[:, t, :], src[:, t, :], mv[:, t, 0:1], rstd[:, t:t + 1],
                                            ALU.subtract, ALU.mult).then_inc(done, 1)

            layer_norm(xtm, xtm, 1, ln_done, x_loaded)
            dve.wait_ge(wv_made, 1)
            nc.vector.tensor_copy(wv[:, :, :], ps[:, 7, 0:KT * 2 * H].rearrange("p (k c) -> p k c", k=KT)).then_inc(wv_copied, 1)
            for t in range(T):
                dve.wait_ge(xw_done, t + 1)
                nc.vector.tensor_copy(ptm[:, t, :], ps[:, 4 + t % 3, 0:F])
                nc.vector.tensor_scalar(f2h[:, t * H:(t + 1) * H], ps[:, 4 + t % 3, F:F + H], 0.5, None, ALU.mult).then_inc(xw_copied, 1)

            def mask_steps(gp, t0, t1):
                with dve.Fori(t0, t1) as t:
                    for s in range(2):
                        dve.wait_ge(exp_done, t * 2 + (gp * T + s + 2))
                        if gp % 2 == 0:
                            dve.wait_ge(mask_loaded[s], (t + (gp // 2 * (T // 2) + 1)) * 16)
                        dve.wait_ge(e_free, gp * T + t * 2 + s + 1)
                        nc.vector.tensor_tensor(
                            buf_e[:, s, :].rearrange("p (h n) -> p h n", h=2),
                            buf_p[:, s, :].rearrange("p (h n) -> p h n", h=2),
                            mask[:, bass.ds(t * 2 + s, 1), :].to_broadcast([P, 2, HALF]),
                            ALU.mult).then_inc(masked, 1)

            def invert(gp):
                dve.wait_ge(den_moved, 32 * (gp + 1))
                link(nc.vector.tensor_scalar(den[:, :], den[:, :], TINY, None, ALU.max))
                nc.vector.reciprocal(den[:, :], den[:, :]).then_inc(inv_ready, 1)

            def normalise(gp):
                dve.wait_ge(inv_spread, 32 * (gp + 1))
                if gp == 0:
                    dve.wait_ge(filled, 16 * -(-S // T))
                half, pair = gp % PASSES // 2, gp % 2
                for h in range(2):
                    q = slice(h * D, (h + 1) * D)
                    nc.vector.tensor_tensor(xc[q, pair, half * HALF:(half + 1) * HALF], raw[q, h, :], invb[q, :],
                                            ALU.mult).then_inc(xc_ready, 1)

            def attention(a):
                for q in range(PASSES):
                    gp = a * PASSES + q
                    if q:
                        mask_steps(gp, 0, 3)
                        invert(gp - 1)
                        mask_steps(gp, 3, 6)
                        normalise(gp - 1)
                        dve.wait_ge(xc_ready, 2 * gp)
                        mask_steps(gp, 6, T // 2)
                    else:
                        mask_steps(gp, 0, T // 2)
                    for b in range(2 * NB):
                        dve.wait_ge(bank_done, 2 * NB * gp + b + 1)
                        nc.vector.tensor_copy(raw[:, b // NB, b % NB * BLK:(b % NB + 1) * BLK], ps[:, b, 0:BLK]).then_inc(raw_copied, 1)
                invert(a * PASSES + PASSES - 1)
                normalise(a * PASSES + PASSES - 1)

            def batch_norm(n, src, g, b):
                for k in range(KT):
                    for c in range(BLOCKS):
                        hi = min((c + 1) * BLK, N)
                        last = nc.vector.bn_stats(bnst[:, k, c, :], src[:, k, c * BLK:hi])
                link(last)
                for k in range(KT):
                    last = nc.vector.bn_aggr(bnmv[:, k, :], bnst[:, k, :, :].rearrange("p a b -> p (a b)"))
                link(last)
                nc.vector.tensor_scalar(bnsc[:, :, 0], bnmv[:, :, 1], BN_EPS, None, ALU.add).then_inc(var_ready, 1)
                dve.wait_ge(std_ready, n)
                link(nc.vector.reciprocal(bnsc[:, :, 1], bnsc[:, :, 0]))
                link(nc.vector.tensor_tensor(bnsc[:, :, 2], bnsc[:, :, 1], vecs[:, g, :], ALU.mult))
                link(nc.vector.tensor_tensor(bnsc[:, :, 1], bnsc[:, :, 2], bnmv[:, :, 0], ALU.mult))
                link(nc.vector.tensor_tensor(bnsc[:, :, 3], vecs[:, b, :], bnsc[:, :, 1], ALU.subtract))
                for k in range(KT):
                    for c in range(2):
                        nc.vector.tensor_scalar(src[:, k, c * HALF:(c + 1) * HALF], src[:, k, c * HALF:(c + 1) * HALF],
                                                bnsc[:, k, 2:3], bnsc[:, k, 3:4], ALU.mult, ALU.add).then_inc(bn_applied, 1)

            def elu(base, dst, res):
                for u in range(UNITS):
                    m, b = u // BLOCKS, u % BLOCKS
                    cols = slice(b * BLK, (b + 1) * BLK)
                    dve.wait_ge(elu_relu, base + u + 1)
                    link(nc.vector.scalar_tensor_tensor(buf_p[:, m, cols], buf_s[:, m, cols], 1.0, buf_p[:, m, cols], ALU.min, ALU.add))
                    if res is None:
                        nc.vector.tensor_scalar(dst[:, m, cols], buf_p[:, m, cols], -1.0, None, ALU.add).then_inc(h_done, 1)
                    else:
                        nc.vector.scalar_tensor_tensor(dst[:, m, cols], buf_p[:, m, cols], -1.0, res[:, m, cols], ALU.add, ALU.add).then_inc(h_done, 1)

            attention(0)
            dve.wait_ge(xc_ready, 2 * PASSES)
            batch_norm(2, xc, ENC_G, ENC_B)
            elu(0, buf_e, xc)
            dve.wait_ge(h_done, UNITS)
            batch_norm(3, buf_e, EM_G, EM_B)
            attention(1)
            elu(UNITS, buf_e, None)
            elu(2 * UNITS, xc, buf_e)
            dve.wait_ge(h_done, 3 * UNITS)
            batch_norm(4, xc, DM_G, DM_B)
            dve.wait_ge(res_loaded, 16)
            for t in range(T):
                dve.wait_ge(ot_done, t + 1)
                last = nc.vector.tensor_tensor(x1[:, t, :], x1[:, t, :], ps[:, t % 8, 0:F], ALU.add).then_inc(x1_done, 1)
            dve.wait_ge(x1_done, T)
            layer_norm(x1, ptm, 5, ln2_done, None)
            dve.wait_ge(lg_done, 1)
            link(nc.vector.tensor_tensor(logits[:, :, :], ps[:, 7, 0:T * E].rearrange("p (t e) -> p t e", e=E),
                                         bg_sb[:, :].rearrange("p (a e) -> p a e", a=1).to_broadcast([P, T, E]), ALU.add))
            for t in range(T):
                last = nc.vector.max(top[:, t, :], logits[:, t, :])
            link(last)
            for t in range(T):
                last = nc.vector.max_index(topi[:, t, :], top[:, t, :], logits[:, t, :])
            link(last)
            nc.vector.tensor_copy(topf[:, :, :], topi[:, :, 0:2])
            nc.vector.tensor_tensor(gate[:, :, 0], top[:, :, 1], top[:, :, 0], ALU.subtract).then_inc(gate_in, 1)
            dve.wait_ge(gate_exp, 1)
            link(nc.vector.tensor_scalar(gate[:, :, 2], gate[:, :, 1], 1.0, None, ALU.add))
            link(nc.vector.reciprocal(gate[:, :, 2], gate[:, :, 2]))
            link(nc.vector.tensor_tensor(gate[:, :, 3], gate[:, :, 2], gate[:, :, 1], ALU.mult))
            dve.wait_ge(tri_made, 2)
            for k in range(2):
                last = nc.vector.tensor_tensor(hot[:, k, :, :], count[:, 0:E].rearrange("p (a e) -> p a e", a=1).to_broadcast([P, T, E]),
                                               topf[:, :, k:k + 1].to_broadcast([P, T, E]), ALU.is_equal)
            link(last)
            nc.vector.tensor_tensor(both[:, :, :], hot[:, 0, :, :], hot[:, 1, :, :], ALU.add).then_inc(hot_ready, 1)
            for k in range(2):
                last = nc.vector.tensor_tensor(pre[:, k, :, :], hot[:, k, :, :], gate[:, :, 2 + k:3 + k].to_broadcast([P, T, E]), ALU.mult)
            link(last)
            nc.vector.tensor_tensor(comb[:, :, :], pre[:, 0, :, :], pre[:, 1, :, :], ALU.add).then_inc(comb_done, 1)
            dve.wait_ge(comb_done, 1)
            dve.wait_ge(pos_done, 1)
            totals = ps[:, 5, 0:T * E].rearrange("p (t e) -> p t e", e=E)
            ranks = ps[:, 4, 0:T * E].rearrange("p (t e) -> p t e", e=E)
            link(nc.vector.tensor_copy(pre[:, 0, :, :], totals))
            cur, d = 0, 1
            while d < T:
                nc.vector.tensor_copy(pre[:, 1 - cur, 0:d, :], pre[:, cur, 0:d, :])
                link(nc.vector.tensor_tensor(pre[:, 1 - cur, d:T, :], pre[:, cur, d:T, :], pre[:, cur, 0:T - d, :], ALU.add))
                cur, d = 1 - cur, 2 * d
            TILES, SUM, FIRST = 0, 1, 3
            full = ps[:, 3, 0:E * T].rearrange("p (e m) -> p e m", e=E)
            past = ps[:, 2, 0:S * E].rearrange("p (s e) -> p s e", e=E)
            eid_f = ps[:, 1, 0:S]
            link(nc.vector.tensor_scalar(ends[:, 5, :], pre[:, cur, T - 1, :], 1.0 / P, None, ALU.mult))
            link(nc.vector.tensor_tensor(full, ends[:, 5, :].rearrange("p (e a) -> p e a", a=1).to_broadcast([P, E, T]),
                                         count[:, 0:T].rearrange("p (a m) -> p a m", a=1).to_broadcast([P, E, T]), ALU.is_gt))
            link(nc.vector.tensor_reduce(ends[:, TILES, :], full, mybir.AxisListType.X, ALU.add))
            link(nc.vector.tensor_copy(ends[:, SUM, :], ends[:, TILES, :]))
            at, d = SUM, 1
            while d < E:
                to = SUM + 1 if at == SUM else SUM
                nc.vector.tensor_copy(ends[:, to, 0:d], ends[:, at, 0:d])
                link(nc.vector.tensor_tensor(ends[:, to, d:E], ends[:, at, d:E], ends[:, at, 0:E - d], ALU.add))
                at, d = to, 2 * d
            link(nc.vector.tensor_tensor(ends[:, FIRST, :], ends[:, at, :], ends[:, TILES, :], ALU.subtract))
            link(nc.vector.tensor_scalar(ends[:, FIRST + 1, :], ends[:, FIRST, :], float(P), None, ALU.mult))
            link(nc.vector.tensor_tensor(pre[:, cur, :, :], pre[:, cur, :, :], totals, ALU.subtract))
            link(nc.vector.tensor_tensor(pre[:, cur, :, :], pre[:, cur, :, :], ranks, ALU.add))
            link(nc.vector.tensor_tensor(pre[:, cur, :, :], pre[:, cur, :, :],
                                         ends[:, FIRST + 1, :].rearrange("p (a e) -> p a e", a=1).to_broadcast([P, T, E]), ALU.add))
            for k in range(2):
                link(nc.vector.tensor_tensor(pre[:, 1 - cur, :, :], pre[:, cur, :, :], hot[:, k, :, :], ALU.mult))
                link(nc.vector.tensor_reduce(slot[:, k, :], pre[:, 1 - cur, :, :], mybir.AxisListType.X, ALU.add))
            nc.vector.tensor_copy(slot_u[:, :, :], slot[:, :, :]).then_inc(slots_ready, 1)
            link(nc.vector.tensor_tensor(past, count[:, :].rearrange("p (s a) -> p s a", a=1).to_broadcast([P, S, E]),
                                         ends[:, at, :].rearrange("p (a e) -> p a e", a=1).to_broadcast([P, S, E]), ALU.is_ge))
            link(nc.vector.tensor_reduce(eid_f, past, mybir.AxisListType.X, ALU.add))
            link(nc.vector.tensor_scalar(eid_f, eid_f, float(E - 1), None, ALU.min))
            nc.vector.tensor_copy(eid[:, :], eid_f).then_inc(slots_ready, 1)
            nc.vector.tensor_scalar(b1s[:, :, :], b1_sb[:, :, :], H_SCALE, None, ALU.mult).then_inc(b1_scaled, 1)
            for w_sb, g, src, n in splits():
                dve.wait_ge(w_high, n + 1)
                at_g = g if w_sb is w1p else g + 1
                nc.vector.scalar_tensor_tensor(w_sb[:, at_g, GRAN:2 * GRAN], src, W_SCALE, w_sb[:, at_g, 0:GRAN],
                                               ALU.mult, ALU.subtract).then_inc(w_low, 1)
            for t in range(T):
                dve.wait_ge(ct_done, t + 1)
                nc.vector.tensor_copy(comb_t[:, (t % 2) * P:(t % 2 + 1) * P], ps[0:E, 4 + t % 2, 0:P]).then_inc(ct_copied, 1)
                dve.wait_ge(b2_done, t + 1)
                nc.vector.tensor_tensor(x1[:, t, :], x1[:, t, :], ps[:, 6, 0:F], ALU.add).then_inc(b2_added, 1)

            def x_half(i, s):
                dve.wait_ge(x_high, i + 1)
                nc.vector.scalar_tensor_tensor(xtp[:, s, 1, :, :].rearrange("p k n -> p (k n)"), ps[:, 6 + s, 0:F], X_SCALE,
                                               xtp[:, s, 0, :, :].rearrange("p k n -> p (k n)"), ALU.mult, ALU.subtract).then_inc(x_low, 1)

            def add_bias(i, s):
                e = nc.vector.value_load(eid[0:1, bass.ds(i, 1)], min_val=0, max_val=E - 1)
                dve.wait_ge(up_done, i + 1)
                wait(dve, h_low, i - 1)
                nc.vector.tensor_tensor(hb[:, s, :].rearrange("p (f n) -> p f n", f=FT),
                                        ps[:, 2 * s:2 * s + 2, :].rearrange("p b (f n) -> p (b f) n", n=P),
                                        b1s[:, bass.ds(e, 1), :].rearrange("p a f -> p (a f)").rearrange("p (f a) -> p f a", a=1).to_broadcast([P, FT, P]),
                                        ALU.add).then_inc(biased, 1)

            def h_half(i, s):
                dve.wait_ge(h_high, i + 1)
                nc.vector.scalar_tensor_tensor(hp[:, s, 1, :, :].rearrange("p f n -> p (f n)"), hb[:, s, :], 0.0,
                                               hp[:, s, 0, :, :].rearrange("p f n -> p (f n)"), ALU.max, ALU.subtract).then_inc(h_low, 1)

            def step(i, s):
                last = isinstance(i, int) and i + 2 >= S
                if not last or i + 1 < S:
                    add_bias(i + 1, 1 - s)
                if not last:
                    x_half(i + 2, s)
                if not last or i + 1 < S:
                    h_half(i + 1, 1 - s)

            dve.wait_ge(slots_ready, 2)
            dve.wait_ge(b1_scaled, 1)
            x_half(0, 0)
            x_half(1, 1)
            add_bias(0, 0)
            h_half(0, 0)
            tiles_in_flight(dve, step)
            for t in range(T):
                for k in range(2):
                    n = 2 * t + k
                    dve.wait_ge(gathered[n % 4], 16 * (n // 4 + 1))
                    if n:
                        dve.wait_ge(combined, n)
                    nc.vector.scalar_tensor_tensor(x1[:, t, :], got[:, n % 4, :], gate[:, t, 2 + k:3 + k], x1[:, t, :],
                                                   ALU.mult, ALU.add).then_inc(combined, 1)

        @block.tensor
        def _(pe):
            pe.sem_inc(e_free, AHEAD)
            pe.wait_ge(ident_made, 1)
            pe.wait_ge(consts_loaded, ALL_CONSTS)
            for k in range(KT):
                last = nc.tensor.matmul(ps[:, 7, k * 2 * H:(k + 1) * 2 * H], wt_bd[:, k, :], v_bd[:, k, :], start=True, stop=True)
            last.then_inc(wv_made, 1)

            def transposes(src, ready, done, copied):
                for t in range(T):
                    pe.wait_ge(ready, t + 1)
                    if t >= 4:
                        pe.wait_ge(copied, t - 3)
                    for k in range(KT):
                        last = nc.tensor.transpose(ps[:, t % 4, k * P:(k + 1) * P], src[:, t, k * P:(k + 1) * P], ident[:, :])
                    last.then_inc(done, 1)

            transposes(xtm, ln_done, tr_done, tr_copied)
            pe.wait_ge(wv_copied, 1)
            for t in range(T):
                pe.wait_ge(tr_copied, t + 1)
                if t >= 3:
                    pe.wait_ge(xw_copied, t - 2)
                for k in range(KT):
                    nc.tensor.matmul(ps[:, 4 + t % 3, k * P:(k + 1) * P], buf_e[:, k, t * P:(t + 1) * P], w_bd[:, k, :], start=True, stop=True)
                for k in range(KT):
                    last = nc.tensor.matmul(ps[:, 4 + t % 3, F:F + H], buf_e[:, k, t * P:(t + 1) * P], wv[:, k, H:2 * H],
                                            start=(k == 0), stop=(k == KT - 1))
                last.then_inc(xw_done, 1)
            for b in range(BLOCKS):
                if b >= 4:
                    pe.wait_ge(f1_copied, b - 3)
                for k in range(KT):
                    last = nc.tensor.matmul(ps[0:H, b % 4, 0:BLK], wv[:, k, 0:H], buf_e[:, k, b * BLK:(b + 1) * BLK],
                                            start=(k == 0), stop=(k == KT - 1))
                last.then_inc(f1_done, 1)

            def product(gp, t, s, first, last_step):
                pe.wait_ge(masked, t * 2 + (gp * T + s + 1 + AHEAD))
                pe.wait_ge(stage_loaded[s], (t + (gp * (T // 2) + 1)) * 16)
                for h in range(2):
                    for b in range(NB):
                        if first and gp:
                            pe.wait_ge(raw_copied, 2 * NB * (gp - 1) + h * NB + b + 1)
                        mm = nc.tensor.matmul(ps[:, h * NB + b, 0:BLK], stage[:, s, h * D:h * D + P],
                                              buf_e[:, s, h * HALF + b * BLK:h * HALF + (b + 1) * BLK],
                                              start=first, stop=last_step)
                        if last_step:
                            mm.then_inc(bank_done, 1)
                if last_step:
                    pe.wait_ge(bank_done, 2 * NB * (gp + 1))
                    pe.sem_inc(e_free, 1)
                else:
                    mm.then_inc(e_free, 1)

            def attention(a):
                for q in range(PASSES):
                    gp = a * PASSES + q
                    product(gp, 0, 0, True, False)
                    product(gp, 0, 1, False, False)
                    with pe.Fori(1, T // 2 - 1) as t:
                        product(gp, t, 0, False, False)
                        product(gp, t, 1, False, False)
                    product(gp, T // 2 - 1, 0, False, False)
                    product(gp, T // 2 - 1, 1, False, True)

            def layer(base, wsb, src, ready, count):
                for u in range(UNITS):
                    m, b = u // BLOCKS, u % BLOCKS
                    if u == 0:
                        pe.wait_ge(ready, count)
                    if u >= 8:
                        pe.wait_ge(elu_relu, base + u - 7)
                    if wsb is wt_bd:
                        mm = nc.tensor.matmul(ps[:, u % 8, 0:BLK], wt_bd_use[:, m, :], src[:, m, b * BLK:(b + 1) * BLK], start=True, stop=True)
                    else:
                        for k in range(KT):
                            mm = nc.tensor.matmul(ps[:, u % 8, 0:BLK], wsb[:, k, m * P:(m + 1) * P], src[:, k, b * BLK:(b + 1) * BLK],
                                                  start=(k == 0), stop=(k == KT - 1))
                    mm.then_inc(z_done, 1)

            wt_bd_use = wt_bd
            attention(0)
            pe.wait_ge(raw_copied, 2 * NB * PASSES)
            layer(0, emw_sb, xc, bn_applied, 4)
            pe.wait_ge(bn_applied, 8)
            for t in range(T // 2):
                if t < 8:
                    pe.wait_ge(elu_relu, UNITS)
                else:
                    pe.wait_ge(et_copied, t - 7)
                for i in range(2):
                    for k in range(KT):
                        last = nc.tensor.transpose(ps[:, t % 8, i * F + k * P:i * F + (k + 1) * P],
                                                   buf_e[:, k, (2 * t + i) * P:(2 * t + i + 1) * P], ident[:, :])
                last.then_inc(et_done, 1)
            pe.wait_ge(et_copied, T // 2)
            attention(1)
            pe.wait_ge(raw_copied, 4 * NB * PASSES)
            layer(UNITS, wt_bd, xc, xc_ready, 4 * PASSES)
            pe.wait_ge(elu_relu, 2 * UNITS)
            layer(2 * UNITS, dmw_sb, buf_e, h_done, 2 * UNITS)
            pe.wait_ge(elu_relu, 3 * UNITS)
            pe.wait_ge(bn_applied, 12)
            for t in range(T):
                if t >= 8:
                    pe.wait_ge(x1_done, t - 7)
                for k in range(KT):
                    last = nc.tensor.transpose(ps[:, t % 8, k * P:(k + 1) * P], xc[:, k, t * P:(t + 1) * P], ident[:, :])
                last.then_inc(ot_done, 1)
            pe.wait_ge(x1_done, T)
            transposes(ptm, ln2_done, tr2_done, tr2_copied)
            pe.wait_ge(tr2_copied, T)
            for t in range(T):
                for k in range(KT):
                    last = nc.tensor.matmul(ps[:, 7, t * E:(t + 1) * E], buf_e[:, k, t * P:(t + 1) * P], wg_sb[:, k, :],
                                            start=(k == 0), stop=(k == KT - 1))
            last.then_inc(lg_done, 1)
            pe.wait_ge(tri_made, 2)
            pe.wait_ge(hot_ready, 1)
            nc.tensor.matmul(ps[:, 4, 0:T * E], before[:, :], both[:, :, :].rearrange("p t e -> p (t e)"), start=True, stop=True)
            nc.tensor.matmul(ps[:, 5, 0:T * E], ones[:, :], both[:, :, :].rearrange("p t e -> p (t e)"), start=True, stop=True).then_inc(pos_done, 1)
            pe.wait_ge(slots_ready, 1)
            pe.wait_ge(comb_done, 1)
            for t in range(T):
                if t >= 2:
                    pe.wait_ge(ct_copied, t - 1)
                nc.tensor.transpose(ps[0:E, 4 + t % 2, 0:P], comb[:, t, :], ident[:, :]).then_inc(ct_done, 1)
                pe.wait_ge(ct_copied, t + 1)
                if t:
                    pe.wait_ge(b2_added, t)
                nc.tensor.matmul(ps[:, 6, 0:F], comb_t[:, (t % 2) * P:(t % 2 + 1) * P], b2_sb[:, :], start=True, stop=True).then_inc(b2_done, 1)
            pe.wait_ge(b2_added, T)
            def transpose_x(i, s):
                pe.wait_ge(xt_loaded[s], half_count(i, s, 1) * 16)
                wait(pe, x_low, i - 1)
                for k in range(KT):
                    last = nc.tensor.transpose(ps[:, 6 + s, k * P:(k + 1) * P], xt[:, s, k * P:(k + 1) * P], ident[:, :])
                last.then_inc(xt_transposed, 1)

            HALVES = ((0, 0), (0, 1), (1, 0))

            def up(i, s):
                e = nc.tensor.value_load(eid[0:1, bass.ds(i, 1)], min_val=0, max_val=E - 1)
                pe.wait_ge(x_low, i + 1)
                wait(pe, biased, i - 1)
                for f in range(FT):
                    for n, (a, b) in enumerate(HALVES):
                        for k in range(KT):
                            g = k * (WG // KT) + f // 4
                            mm = nc.tensor.matmul(ps[:, 2 * s + f // 4, f % 4 * P:(f % 4 + 1) * P],
                                                  w1p[:, bass.ds(e * WG + g, 1), a * GRAN + f % 4 * P:a * GRAN + (f % 4 + 1) * P]
                                                  .rearrange("p a c -> p (a c)"),
                                                  xtp[:, s, b, k, :], start=(n == 0 and k == 0), stop=(n == 2 and k == KT - 1))
                mm.then_inc(up_done, 1)

            def down(i, s):
                e = nc.tensor.value_load(eid[0:1, bass.ds(i, 1)], min_val=0, max_val=E - 1)
                pe.wait_ge(h_low, i + 1)
                wait(pe, y_copied, i - 1)
                for n, (a, b) in enumerate(HALVES):
                    for f in range(FT):
                        mm = nc.tensor.matmul(ps[:, 4 + s, 0:F], hp[:, s, b, f, :],
                                              w2p[:, bass.ds(e * WG + f // 2 + 1, 1), a * GRAN + f % 2 * F:a * GRAN + (f % 2 + 1) * F]
                                              .rearrange("p a c -> p (a c)"),
                                              start=(n == 0 and f == 0), stop=(n == 2 and f == FT - 1))
                mm.then_inc(down_done, 1)

            def step(i, s):
                last = isinstance(i, int) and i + 2 >= S
                if not last:
                    transpose_x(i + 2, s)
                if not last or i + 1 < S:
                    up(i + 1, 1 - s)
                down(i, s)

            pe.wait_ge(slots_ready, 2)
            pe.wait_ge(w_low, 2 * E * WG)
            transpose_x(0, 0)
            transpose_x(1, 1)
            up(0, 0)
            tiles_in_flight(pe, step)


_OUT = ("out_dram", (N, F))


def kernel(x, adj, L0_gnn_W, L0_gnn_V, L0_gnn_enc_bn_gamma, L0_gnn_enc_bn_beta, L0_gnn_enc_mlp_W, L0_gnn_enc_mlp_b,
           L0_gnn_enc_mlp_bn_gamma, L0_gnn_enc_mlp_bn_beta, L0_gnn_dec_mlp_W, L0_gnn_dec_mlp_b,
           L0_gnn_dec_mlp_bn_gamma, L0_gnn_dec_mlp_bn_beta, L0_ffn_Wg, L0_ffn_bg, L0_ffn_W1, L0_ffn_b1,
           L0_ffn_W2, L0_ffn_b2):
    import numpy as np
    import concourse.bacc as bacc
    from concourse.bass_utils import run_bass_kernel_spmd

    xp = np.zeros((NP, F), np.float32)
    xp[:N] = np.asarray(x)
    adj_t = np.zeros((NP, NP), np.float32)
    adj_t[:N, :N] = np.asarray(adj).T
    w = np.asarray(L0_gnn_W)
    host = {
        "x": xp, "adj_t": adj_t, "w": w, "wt": w.transpose(0, 2, 1), "v": L0_gnn_V,
        "enc_g": L0_gnn_enc_bn_gamma, "enc_b": L0_gnn_enc_bn_beta,
        "emw_t": np.asarray(L0_gnn_enc_mlp_W).T, "emb": L0_gnn_enc_mlp_b,
        "em_g": L0_gnn_enc_mlp_bn_gamma, "em_b": L0_gnn_enc_mlp_bn_beta,
        "dmw_t": np.asarray(L0_gnn_dec_mlp_W).T, "dmb": L0_gnn_dec_mlp_b,
        "dm_g": L0_gnn_dec_mlp_bn_gamma, "dm_b": L0_gnn_dec_mlp_bn_beta,
        "wg": L0_ffn_Wg, "bg": L0_ffn_bg, "w1": L0_ffn_W1, "b1": L0_ffn_b1, "w2": L0_ffn_W2, "b2": L0_ffn_b2,
    }
    nc = bacc.Bacc("TRN2", target_bir_lowering=False, num_devices=1)
    arrays, args = {}, {}
    for name, a in host.items():
        a = np.ascontiguousarray(np.asarray(a))
        arrays[f"in_{name}"] = a
        args[name] = nc.dram_tensor(f"in_{name}", a.shape, mybir.dt.from_np(a.dtype), kind="ExternalInput").ap()
    out = nc.dram_tensor(_OUT[0], _OUT[1], F32, kind="ExternalOutput").ap()
    build(nc, out=out, **args)
    r = run_bass_kernel_spmd(nc, [arrays], core_ids=[0])
    return r.results[0][_OUT[0]]
```

```python
from contextlib import ExitStack

import concourse.bass as bass
from concourse import mybir

F32 = mybir.dt.float32
U8 = mybir.dt.uint8
U32 = mybir.dt.uint32
I32 = mybir.dt.int32
F16 = mybir.dt.float16
ALU = mybir.AluOpType
ACT = mybir.ActivationFunctionType

P = 128
N = 3327
T = -(-N // P)
NP = T * P
F = 256
KT = F // P
H = 4
D = F // H
HALF = NP // 2
NB = 4
BLK = HALF // NB
BLOCKS = 2 * NB
PASSES = 4
E = 8
FF = 1024
FT = FF // P
PAIRS = 2 * T
S = PAIRS + E
GRAN = 512
WG = KT * FF // GRAN
XRING = 4
FIRST = 2
W2_EARLY = 12
PACKED = XRING + 2
E_BITS = (E - 1).bit_length()
CHUNK = 4
W_SCALE = 64.0
X_SCALE = 4.0
H_SCALE = W_SCALE * X_SCALE
Y_SCALE = H_SCALE * W_SCALE
LN_EPS = 1e-5
BN_EPS = 1e-6
TINY = 1e-30
BN_PARTS = 4
BN_COLS = NP // BN_PARTS
X_ENDS = (0, 4, 9, 17, T)
AHEAD = 2


def build(nc, x, adj_t, w, wt, v, enc_g, enc_b, emw_t, emb, em_g, em_b, dmw_t, dmb, dm_g, dm_b,
          wg, bg, w1, b1, w2, b2, out):
    xw_dram = nc.dram_tensor("xw_scratch", [NP, F], F32, kind="Internal").ap()
    f1_dram = nc.dram_tensor("f1_scratch", [H, NP], F32, kind="Internal").ap()
    xn_dram = nc.dram_tensor("expert_input_scratch", [NP + P, F], F32, kind="Internal").ap()
    b2_dram = nc.dram_tensor("b2_scratch", [2, E * F], F16, kind="Internal").ap()
    inv_dram = nc.dram_tensor("inv_scratch", [2 * PASSES, 2, HALF], F32, kind="Internal").ap()

    with ExitStack() as ctx:
        def sb(name, shape, dt=F32, scope=ctx):
            return scope.enter_context(nc.sbuf_tensor(name, shape, dt))

        def sem(name):
            return ctx.enter_context(nc.semaphore(name))

        ident = sb("ident", [P, P])
        w_bd = sb("w_bd", [P, KT, P + 2])
        wt_bd = sb("wt_bd", [P, KT, P])
        v_bd = sb("v_bd", [P, KT, 2 * H])
        wv = sb("wv", [P, KT, 2 * H])
        emw_sb = sb("emw_sb", [P, KT, F])
        dmw_sb = sb("dmw_sb", [P, KT, F])
        vecs = sb("vecs", [P, 8, KT])
        ENC_G, ENC_B, EMB, EM_G, EM_B, DMB, DM_G, DM_B = range(8)
        bg_sb = sb("bg_sb", [P, E])
        wg_sb = sb("wg_sb", [P, KT, E])
        b1_sb = sb("b1_sb", [P, E, FT])
        f2h = sb("f2h", [P, T * H])
        stats = sb("stats", [P, T, 6])
        mv = sb("mv", [P, T, 2])
        rstd = sb("rstd", [P, T])
        bnst = sb("bnst", [P, KT, BLOCKS, 6])
        bnmv = sb("bnmv", [P, KT, 2])
        bnsc = sb("bnsc", [P, KT, 4])
        den = sb("den", [P, 2 * HALF // P])
        b1s = sb("b1s", [P, E, FT])

        stage = sb("stage", [P, 2, 3 * D])

        with ExitStack() as later:
            x1 = sb("x1", [P, T, F], F32, later)
            w1p = sb("w1p", [P, E * WG + 1, 2 * GRAN], F16, later)
        mask = sb("mask", [P, T, HALF], U8)
        f1b = sb("f1b", [P, 2, 2, HALF])
        raw = sb("raw", [P, 2, HALF])
        invb = sb("invb", [P, HALF])
        sb("pad", [P, (T * F * 4 + (E * WG + 1) * GRAN * 4 - T * HALF - 7 * HALF * 4) // 4])
        with ExitStack() as later:
            xt = sb("xt", [P, XRING, F], F32, later)
            xtp = sb("xtp", [P, 2, 2, KT, P], F16, later)
            hb = sb("hb", [P, FT * P], F32, later)
            hp = sb("hp", [P, 2, 2, FT, P], F16, later)
            ysb = sb("ysb", [P, 2, F], F32, later)
            b2p = sb("b2p", [2, E * F], F16, later)
            used = XRING * F + 2 * KT * P + FT * P + 2 * FT * P + 2 * F + E * F // 2
            sb("pad_p", [P, 2 * NP - used], F32, later)
            w2p = sb("w2p", [P, E * WG + 1, 2 * GRAN], F16, later)
            logits = sb("logits", [P, T, E], F32, later)
            top = sb("top", [P, T, 8], F32, later)
            topi = sb("topi", [P, T, 8], U32, later)
            topf = sb("topf", [P, T, 2], F32, later)
            count_u = sb("count_u", [P, P], U32, later)
            count = sb("count", [P, P], F32, later)
            node_u = sb("node_u", [P, 2, T], U32, later)
            node = sb("node", [P, 2, T], F32, later)
            gate = sb("gate", [P, 4, T], F32, later)
            hot = sb("hot", [P, 2, T, E], F32, later)
            both = sb("both", [P, T, E], F32, later)
            pre = sb("pre", [P, 2, T, E], F32, later)
            ends = sb("ends", [P, 6, E], F32, later)
            slot = sb("slot", [P, 2 * T], F32, later)
            slot_i = sb("slot_i", [P, 3, 2 * T], I32, later)
            place = sb("place", [P, 2, 2 * T], F32, later)
            spare = sb("spare", [P, 2], F32, later)
            free = sb("free", [P, S], F32, later)
            node_of = sb("node_of", [P, S], U32, later)
            gate_of = sb("gate_of", [P, S], F32, later)
            eids = sb("eids", [P, S], I32, later)
            before = sb("before", [P, P], F32, later)
            ones = sb("ones", [P, P], F32, later)
            ones2 = sb("ones2", [2, P], F16, later)
        with ExitStack() as later:
            tile_hot = sb("tile_hot", [P, 2, CHUNK, 3, S], F32, later)
            col_hot = sb("col_hot", [P, 2, CHUNK, P], F32, later)
            assert 2 * CHUNK * (3 * S + P) <= 2 * NP
        buf_p = sb("buf_p", [P, 2, NP])
        buf_e = sb("buf_e", [P, 2, NP])
        buf_s = sb("buf_s", [P, 2, NP])
        xc = sb("xc", [P, KT, NP])

        ps = ctx.enter_context(nc.psum_tensor("ps", [P, 8, 512], F32))

        x_loaded = [sem(f"x_loaded{i}") for i in range(len(X_ENDS) - 1)]
        consts_loaded = sem("consts_loaded")
        zeroed = sem("zeroed")
        ident_made = sem("ident_made")
        wv_made = sem("wv_made")
        wv_copied = sem("wv_copied")
        dve_step = sem("dve_step")
        var_ready = sem("var_ready")
        std_ready = sem("std_ready")
        ln_done = sem("ln_done")
        tr_done = sem("tr_done")
        tr_copied = sem("tr_copied")
        xw_done = sem("xw_done")
        xw_copied = sem("xw_copied")
        f1_done = sem("f1_done")
        f1_copied = sem("f1_copied")
        f1_stored = sem("f1_stored")
        xw_stored = sem("xw_stored")
        f1b_loaded = [sem(f"f1b_loaded{i}") for i in range(2)]
        stage_loaded = [sem(f"stage_loaded{i}") for i in range(2)]
        mask_loaded = [sem(f"mask_loaded{i}") for i in range(2)]
        tanh_done = sem("tanh_done")
        exp_done = sem("exp_done")
        masked = sem("masked")
        e_free = sem("e_free")
        bank_done = sem("bank_done")
        raw_copied = sem("raw_copied")
        den_moved = [sem(f"den_moved{i}") for i in range(2)]
        inv_ready = sem("inv_ready")
        inv_stored = [sem(f"inv_stored{i}") for i in range(2)]
        inv_spread = [sem(f"inv_spread{i}") for i in range(2)]
        xc_ready = sem("xc_ready")
        bn_applied = sem("bn_applied")
        z_done = sem("z_done")
        elu_relu = sem("elu_relu")
        h_done = sem("h_done")
        et_done = sem("et_done")
        et_copied = sem("et_copied")
        emb_stored = sem("emb_stored")
        res_loaded = sem("res_loaded")
        ot_done = sem("ot_done")
        x1_done = sem("x1_done")
        ln2_done = sem("ln2_done")
        tr2_done = sem("tr2_done")
        tr2_copied = sem("tr2_copied")
        lg_done = sem("lg_done")
        gate_exp = sem("gate_exp")
        gate_in = sem("gate_in")
        small_free = sem("small_free")
        tri_made = sem("tri_made")
        hot_ready = sem("hot_ready")
        pos_done = sem("pos_done")
        slots_ready = sem("slots_ready")
        xn_stored = sem("xn_stored")
        hots_made = sem("hots_made")
        hots_used = sem("hots_used")
        map_ready = sem("map_ready")
        b2_split = sem("b2_split")
        b2_stored = sem("b2_stored")
        b2_loaded = sem("b2_loaded")
        out_written = sem("out_written")
        w1_staged = [sem(f"w1_staged{e}") for e in range(E)]
        w2_staged = [sem(f"w2_staged{e}") for e in range(E)]
        w1_high = sem("w1_high")
        w1_low = sem("w1_low")
        w2_high = sem("w2_high")
        w2_low = sem("w2_low")
        w2_scaled = sem("w2_scaled")
        b1_scaled = sem("b1_scaled")
        xt_loaded = [sem(f"xt_loaded{i}") for i in range(XRING)]
        xt_transposed = sem("xt_transposed")
        x_high = sem("x_high")
        x_low = sem("x_low")
        up_done = sem("up_done")
        biased = sem("biased")
        h_high = sem("h_high")
        h_low = sem("h_low")
        down_done = sem("down_done")
        y_high = sem("y_high")
        y_copied = sem("y_copied")
        added = sem("added")

        def index(i, more=0):
            return i[0] * XRING + (i[1] + more)

        def rounds(i, ring, more=0):
            return i[0] * (XRING // ring) + (i[1] // ring + more)

        def ahead(i, k):
            return i[0], i[1] + k

        def exists(i):
            return not isinstance(i[0], int) or 0 <= index(i) < S

        def wait(eng, semaphore, value):
            if not isinstance(value, int) or value > 0:
                eng.wait_ge(semaphore, value)

        def each_tile(eng, step, start=None):
            if start:
                start((0, 0), FIRST + 2)
            for c in range(FIRST):
                step((0, c))
            with eng.Fori(0, (S - FIRST - 3) // XRING) as n:
                if start:
                    start((n, FIRST), XRING + 2)
                for c in range(XRING):
                    step((n, c + FIRST))
            rest = FIRST + (S - FIRST - 3) // XRING * XRING
            if start:
                start((0, rest), S - rest)
            for c in range(rest, S):
                step((0, c))

        xtm = buf_s[:, :, :].rearrange("p a n -> p (a n)").rearrange("p (t f) -> p t f", f=F)
        ptm = buf_p[:, :, :].rearrange("p a n -> p (a n)").rearrange("p (t f) -> p t f", f=F)
        xw_tm = xc[:, :, :].rearrange("p a n -> p (a n)").rearrange("p (t f) -> p t f", f=F)
        b2row = f1b[0:1, 1, :, :].rearrange("p a n -> p (a n)")[:, 0:E * F]
        b2high = f1b[0:1, 1, :, :].rearrange("p a n -> p (a n)")[:, E * F:E * F * 3 // 2].bitcast(F16)
        b2low = invb[0:1, 0:E * F // 2].bitcast(F16)
        f1row = raw[0:H, :, :].rearrange("p a n -> p (a n)")
        x_tm = x.rearrange("(t p) f -> p t f", p=P)

        consts = []
        for h in range(H):
            q = slice((h % 2) * D, (h % 2) * D + D)
            consts.append((w_bd[q, h // 2, q], w[h]))
            consts.append((wt_bd[q, h // 2, q], wt[h]))
            for k in range(2):
                consts.append((v_bd[q, h // 2, H * k + h:H * k + h + 1], v[h, k]))
        for n, a in enumerate((enc_g, enc_b, emb, em_g, em_b, dmb, dm_g, dm_b)):
            consts.append((vecs[:, n, :], a.rearrange("(t p) -> p t", p=P)))
        consts += [(emw_sb[:, :, :], emw_t.rearrange("(t p) o -> p t o", p=P)),
                   (dmw_sb[:, :, :], dmw_t.rearrange("(t p) o -> p t o", p=P)),
                   (wg_sb[:, :, :], wg.rearrange("(t p) e -> p t e", p=P)),
                   (b1_sb[:, :, :], b1.rearrange("e (t p) -> p e t", p=P)),
                   (b2row, b2.rearrange("(a e) f -> a (e f)", a=1)),
                   (bg_sb[:, :], bg.rearrange("(a e) -> a e", a=1).to_broadcast([P, E]))]
        ALL_CONSTS = 16 * len(consts)
        STEPS = T * PASSES
        UNITS = KT * BLOCKS

        decoder = [(1, m, 0) for m in range(KT)]
        for b in range(BLOCKS):
            decoder += [(1, m, b + 1) for m in range(KT) if b + 1 < BLOCKS] + [(2, m, b) for m in range(KT)]

        def applied(n, nodes):
            return KT * (n * BN_PARTS + -(-nodes // BN_COLS))

        def w_piece(w_sb, k):
            if w_sb is w1p:
                return w1p[:, k + 1, :].bitcast(F32), w1p[:, k, 0:GRAN], w1p[:, k, GRAN:2 * GRAN]
            g = E * WG - 1 - k
            rows = w2p[:, g + 1, :].rearrange("p (t a f) -> p t a f", a=2, f=F)
            return w2p[:, g, :].bitcast(F32).rearrange("p (t f) -> p t f", f=F), rows[:, :, 0, :], rows[:, :, 1, :]

        def inverse_by(gp):
            a, q = gp // PASSES, gp % PASSES
            return (1, a + 1) if q == PASSES - 1 else (0, a * (PASSES - 1) + q + 1)

        def spread_inverse(queue, gp):
            i, times = inverse_by(gp)
            queue.wait_ge(raw_copied, 2 * NB * (gp + 1))
            for h in range(2):
                row = D * (1 - h)
                queue.dma_start(den[:, h * (HALF // P):(h + 1) * (HALF // P)],
                                raw[row:row + 1, h, :]).then_inc(den_moved[i], 16)
            queue.wait_ge(inv_ready, gp + 1)
            for h in range(2):
                queue.dma_start(inv_dram[gp, h].rearrange("(p c) -> p c", p=P),
                                den[:, h * (HALF // P):(h + 1) * (HALF // P)]).then_inc(inv_stored[i], 16)
            queue.wait_ge(inv_stored[i], 32 * times)
            for h in range(2):
                queue.dma_start(invb[h * D:(h + 1) * D, :],
                                inv_dram[gp, h:h + 1].to_broadcast([D, HALF])).then_inc(inv_spread[i], 16)

        block = ctx.enter_context(nc.Block())

        @block.sync
        def _(sp):
            for i, (t0, t1) in enumerate(zip(X_ENDS, X_ENDS[1:])):
                sp.dma_start(xtm[:, t0:t1, :], x_tm[:, t0:t1, :]).then_inc(x_loaded[i], 16)
            sp.wait_ge(zeroed, 3)
            with nc.allow_non_contiguous_dma(reason="small vectors"):
                for dst, src in consts:
                    sp.dma_start(dst, src).then_inc(consts_loaded, 16)
            sp.wait_ge(b2_split, 2)
            sp.dma_start(b2_dram[0:1, :], b2high).then_inc(b2_stored, 16)
            sp.dma_start(b2_dram[1:2, :], b2low).then_inc(b2_stored, 16)
            sp.wait_ge(b2_stored, 32)
            sp.wait_ge(f1_copied, BLOCKS)
            sp.dma_start(f1_dram, f1row).then_inc(f1_stored, 16)

            def load_f1(gp):
                half, pair = gp % PASSES // 2, gp % 2
                if gp >= 2:
                    sp.wait_ge(tanh_done, 2 * T * (gp - 1))
                src = f1_dram[2 * pair:2 * pair + 2, half * HALF:(half + 1) * HALF]
                sp.dma_start(f1b[:, gp % 2, :, :], src.rearrange("(a h) n -> a h n", a=1).to_broadcast([P, 2, HALF])) \
                    .then_inc(f1b_loaded[gp % 2], 16)

            def load_w1(e):
                dst = w1p[:, e * WG + 1:(e + 1) * WG + 1, :].rearrange("p g c -> p (g c)").bitcast(F32)
                sp.dma_start(dst.rearrange("p (k f) -> p k f", k=KT), w1[e].rearrange("(k p) f -> p k f", p=P)).then_inc(w1_staged[e], 16)

            sp.wait_ge(f1_stored, 16)
            load_f1(0)
            ends = (0, T // 3, 2 * T // 3, T - 3, T)
            for t0, t1 in zip(ends, ends[1:]):
                sp.wait_ge(xw_copied, t1)
                sp.dma_start(xw_dram.rearrange("(t p) f -> p t f", p=P)[:, t0:t1, :],
                             xw_tm[:, t0:t1, :]).then_inc(xw_stored, 16)
            sp.wait_ge(xw_stored, 64)
            for gp in range(2 * PASSES):
                pair = gp % 2
                if gp + 1 < 2 * PASSES:
                    load_f1(gp + 1)
                if gp == PASSES:
                    sp.wait_ge(emb_stored, 64)
                with sp.Fori(0, T // 2) as t:
                    for s in range(2):
                        sp.wait_ge(e_free, gp * T + t * 2 + s + 1)
                        sp.dma_start(
                            stage[:, s, :].rearrange("p (c d) -> p c d", d=D)[:, 0:3:2, :],
                            xw_dram[bass.ds(t * (2 * P) + s * P, P), pair * P:(pair + 1) * P]
                            .rearrange("p (c d) -> p c d", d=D)).then_inc(stage_loaded[s], 16)
                if gp == 2 * PASSES - 1:
                    sp.wait_ge(masked, 2 * STEPS + AHEAD)
                    load_w1(0)
                if gp % PASSES == PASSES - 1:
                    spread_inverse(sp, gp)
                if gp == PASSES - 1:
                    for t0, t1 in zip(ends, ends[1:]):
                        sp.wait_ge(et_copied, -(-t1 // 2))
                        sp.dma_start(xw_dram.rearrange("(t p) f -> p t f", p=P)[:, t0:t1, :],
                                     xw_tm[:, t0:t1, :]).then_inc(emb_stored, 16)
            sp.wait_ge(xc_ready, 4 * PASSES)
            sp.dma_start(x1[:, :, :], x_tm).then_inc(res_loaded, 16)
            for e in range(1, E):
                load_w1(e)
            for e in reversed(range(E)):
                if e == E - 1:
                    sp.wait_ge(h_done, 3 * UNITS)
                    sp.wait_ge(x1_done, T)
                if e == E // 2 - 1:
                    sp.dma_start(out[0:NP, :].rearrange("(t p) f -> p t f", p=P), x1[:, :, :]).then_inc(out_written, 16)
                    sp.dma_start(out[NP:NP + P, :], x1[:, 0, :]).then_inc(out_written, 16)
                    sp.wait_ge(ln2_done, T)
                    sp.dma_start(xn_dram[0:NP, :].rearrange("(t p) f -> p t f", p=P), ptm).then_inc(xn_stored, 16)
                    sp.dma_start(xn_dram[NP:NP + P, :], ptm[:, 0, :]).then_inc(xn_stored, 16)
                    sp.wait_ge(lg_done, 1)
                dst = w2p[:, e * WG:(e + 1) * WG, :].rearrange("p g c -> p (g c)").bitcast(F32)
                sp.dma_start(dst.rearrange("p (t f) -> p t f", t=FT), w2[e].rearrange("(t p) f -> p t f", p=P)).then_inc(w2_staged[e], 16)
            sp.wait_ge(map_ready, 1)
            sp.dma_start(b2p[:, :], b2_dram).then_inc(b2_loaded, 16)

        @block.gpsimd
        def _(pool):
            nc.gpsimd.memset(w_bd[:, :, :], 0.0).then_inc(zeroed, 1)
            nc.gpsimd.memset(wt_bd[:, :, :], 0.0).then_inc(zeroed, 1)
            nc.gpsimd.memset(v_bd[:, :, :], 0.0).then_inc(zeroed, 1)
            nc.gpsimd.memset(ident[:, :], 0.0).then_inc(zeroed, 1)
            nc.gpsimd.memset(stage[:, :, :], 1.0).then_inc(zeroed, 1)
            pool.wait_ge(zeroed, 5)
            nc.gpsimd.affine_select(out=ident[:, :], in_=ident[:, :], compare_op=ALU.not_equal, fill=1.0,
                                    base=0, pattern=[[-1, P]], channel_multiplier=1).then_inc(ident_made, 1)

            def load_masks(count, half, after):
                def load_pair(t):
                    for s in range(2):
                        if after is not None:
                            pool.wait_ge(masked, t * 2 + (after + s + 1 + AHEAD))
                        if count or not isinstance(t, int):
                            pool.wait_ge(mask_loaded[s], (t + count * (T // 2)) * 16)
                        pool.dma_start(mask[:, bass.ds(t * 2 + s, 1), :].rearrange("p a n -> p (a n)"),
                                       adj_t[bass.ds(t * (2 * P) + s * P, P), half * HALF:(half + 1) * HALF]) \
                            .then_inc(mask_loaded[s], 16)

                load_pair(0)
                with pool.Fori(1, T // 2) as t:
                    load_pair(t)

            load_masks(0, 0, None)
            for gp in range(2 * PASSES):
                if gp % PASSES:
                    spread_inverse(pool, gp - 1)
                if gp % 2 and gp + 1 < 2 * PASSES:
                    load_masks((gp + 1) // 2, (gp // 2 + 1) % 2, gp * T)

            pool.wait_ge(x1_done, T)
            nc.gpsimd.iota(count_u[:, :], [[1, P]], base=0, channel_multiplier=0).then_inc(small_free, 1)
            nc.gpsimd.iota(node_u[:, :, :], [[0, 2], [P, T]], base=0, channel_multiplier=1).then_inc(small_free, 1)
            nc.gpsimd.memset(ones[:, :], 1.0).then_inc(small_free, 1)
            nc.gpsimd.memset(ones2[:, :], H_SCALE).then_inc(small_free, 1)
            pool.wait_ge(small_free, 4)
            nc.gpsimd.tensor_copy(count[:, :], count_u[:, :]).then_inc(tri_made, 1)
            nc.gpsimd.tensor_copy(node[:, :, :], node_u[:, :, :]).then_inc(tri_made, 1)
            nc.gpsimd.affine_select(out=before[:, :], in_=ones[:, :], compare_op=ALU.is_gt, fill=0.0,
                                    base=0, pattern=[[1, P]], channel_multiplier=-1).then_inc(tri_made, 1)
            pool.wait_ge(tri_made, 3)
            nc.gpsimd.tensor_scalar(spare[:, 0:1], node[:, 0, 0:1], float(NP), None, ALU.add).then_inc(small_free, 1)
            pool.wait_ge(small_free, 5)
            nc.gpsimd.tensor_scalar(spare[:, 1:2], spare[:, 0:1], -1.0, None, ALU.mult).then_inc(small_free, 1)

            for k in range(W2_EARLY, E * WG):
                src, high, low = w_piece(w2p, k)
                pool.wait_ge(w2_high, k + 1)
                nc.gpsimd.tensor_tensor(low, src, high, ALU.subtract).then_inc(w2_low, 1)

            def gather(i):
                if i >= XRING:
                    pool.wait_ge(xt_transposed, i - XRING + 1)
                nc.gpsimd.indirect_dma_start(
                    out=xt[:, i % XRING, :], out_offset=None,
                    in_=xn_dram, in_offset=bass.IndirectOffsetOnAxis(ap=node_of[:, i:i + 1], axis=0),
                    bounds_check=NP + P - 1, oob_is_err=True).then_inc(xt_loaded[i % XRING], 16)

            pool.wait_ge(xn_stored, 32)
            pool.wait_ge(out_written, 32)
            pool.wait_ge(map_ready, 1)
            for i in range(XRING):
                gather(i)
            for i in range(S):
                if i + XRING < S:
                    gather(i + XRING)
                pool.wait_ge(y_copied, i + 1)
                if i:
                    pool.wait_ge(added, 16 * i)
                nc.gpsimd.indirect_dma_start(
                    out=out, out_offset=bass.IndirectOffsetOnAxis(ap=node_of[:, i:i + 1], axis=0),
                    in_=ysb[:, i % 2, :], in_offset=None, compute_op=ALU.add,
                    bounds_check=NP + P - 1, oob_is_err=True).then_inc(added, 16)
            pool.wait_ge(added, 16 * S)

        @block.scalar
        def _(act):
            act.sem_inc(exp_done, 1)
            act.wait_ge(var_ready, 1)
            nc.scalar.activation(rstd[:, :], rstd[:, :], ACT.Sqrt).then_inc(std_ready, 1)

            def copy_transposed(t, done, copied, dst):
                act.wait_ge(done, t + 1)
                nc.scalar.activation(dst[:, :, t * P:(t + 1) * P],
                                     ps[:, t % 4, 0:F].rearrange("p (k n) -> p k n", k=KT), ACT.Copy).then_inc(copied, 1)

            for t in range(T):
                copy_transposed(t, tr_done, tr_copied, buf_e)
            for b in range(BLOCKS):
                act.wait_ge(f1_done, b + 1)
                nc.scalar.activation(f1row[:, b * BLK:(b + 1) * BLK], ps[0:H, b % 4, 0:BLK], ACT.Copy).then_inc(f1_copied, 1)

            def tanh(gp, jt, s, h):
                if h == 0:
                    act.wait_ge(exp_done, jt + gp * T if gp or not isinstance(jt, int) else max(jt, 1))
                col = jt * H + (gp % 2) * 2 + h
                nc.scalar.activation(buf_s[:, s, h * HALF:(h + 1) * HALF], f1b[:, gp % 2, h, :], ACT.Tanh,
                                     bias=f2h[:, bass.ds(col, 1)], scale=0.5).then_inc(tanh_done, 1)

            def exp(step, s):
                act.wait_ge(tanh_done, step * 2 + 2)
                act.wait_ge(masked, step + 1)
                nc.scalar.activation(buf_p[:, s, :], buf_s[:, s, :], ACT.Exp, scale=0.5).then_inc(exp_done, 1)

            def attention(a):
                for q in range(PASSES):
                    gp = a * PASSES + q
                    g0 = gp * T
                    if q == 0:
                        act.wait_ge(f1b_loaded[gp % 2], 16 * (gp // 2 + 1))
                        if gp == 0:
                            act.wait_ge(xw_copied, 1)
                        tanh(gp, 0, 0, 0)
                    tanh(gp, 0, 0, 1)
                    if gp == 0:
                        act.wait_ge(xw_copied, T)
                    with act.Fori(0, T // 2 - 1) as t:
                        tanh(gp, t * 2 + 1, 1, 0)
                        exp(t * 2 + g0, 0)
                        tanh(gp, t * 2 + 1, 1, 1)
                        tanh(gp, t * 2 + 2, 0, 0)
                        exp(t * 2 + (g0 + 1), 1)
                        tanh(gp, t * 2 + 2, 0, 1)
                    tanh(gp, T - 1, 1, 0)
                    exp(g0 + T - 2, 0)
                    tanh(gp, T - 1, 1, 1)
                    if q < PASSES - 1:
                        act.wait_ge(f1b_loaded[(gp + 1) % 2], 16 * ((gp + 1) // 2 + 1))
                        tanh(gp + 1, 0, 0, 0)
                    exp(g0 + T - 1, 1)

            def bn_sqrt(n):
                act.wait_ge(var_ready, n + 1)
                nc.scalar.activation(bnsc[:, :, 0], bnsc[:, :, 0], ACT.Sqrt).then_inc(std_ready, 1)

            def w1_high_half(k):
                src, high, _ = w_piece(w1p, k)
                act.wait_ge(w1_staged[k // WG], 16)
                if k:
                    act.wait_ge(w1_low, k)
                nc.scalar.activation(high, src, ACT.Copy, scale=W_SCALE).then_inc(w1_high, 1)

            def w2_high_half(k, scale):
                src, high, _ = w_piece(w2p, k)
                act.wait_ge(w2_staged[(E * WG - 1 - k) // WG], 16)
                if k:
                    act.wait_ge(w2_low, k)
                nc.scalar.activation(high, src, ACT.Copy, scale=scale).then_inc(w2_high, 1)

            def scale_w2(k):
                src = w_piece(w2p, k)[0]
                act.wait_ge(w2_staged[(E * WG - 1 - k) // WG], 16)
                nc.scalar.activation(src, src, ACT.Copy, scale=W_SCALE).then_inc(w2_scaled, 1)

            def elu_parts(n, m, b, bias):
                cols = slice(b * BLK, (b + 1) * BLK)
                act.wait_ge(z_done, n + 1)
                z = ps[:, n % 8, 0:BLK]
                bb = 0.0 if bias is None else vecs[:, bias, m:m + 1]
                nc.scalar.activation(buf_s[:, m, cols], z, ACT.Exp, bias=bb)
                nc.scalar.activation(buf_p[:, m, cols], z, ACT.Relu, bias=bb).then_inc(elu_relu, 1)

            attention(0)
            bn_sqrt(1)
            for u in range(UNITS):
                elu_parts(u, u // BLOCKS, u % BLOCKS, EMB)
            bn_sqrt(2)
            for t in range(T // 2):
                act.wait_ge(et_done, t + 1)
                nc.scalar.activation(xw_tm[:, 2 * t:2 * t + 2, :], ps[:, t % 8, :].rearrange("p (t f) -> p t f", f=F),
                                     ACT.Copy).then_inc(et_copied, 1)
            attention(1)
            for k in range(WG):
                w1_high_half(k)
            pieces = WG
            for n, (which, m, b) in enumerate(decoder):
                elu_parts(UNITS + n, m, b, None if which == 1 else DMB)
                if which == 2:
                    w1_high_half(pieces)
                    pieces += 1
            bn_sqrt(3)
            act.wait_ge(var_ready, 5)
            nc.scalar.activation(rstd[:, :], rstd[:, :], ACT.Sqrt).then_inc(std_ready, 1)
            for t in range(T):
                copy_transposed(t, tr2_done, tr2_copied, buf_e)
            for k in range(E * WG - WG - UNITS):
                w1_high_half(WG + UNITS + k)
                if k < W2_EARLY:
                    w2_high_half(k, W_SCALE)
            act.wait_ge(gate_in, 1)
            nc.scalar.activation(gate[:, 1, :], gate[:, 0, :], ACT.Exp).then_inc(gate_exp, 1)
            scale_w2(W2_EARLY)
            for k in range(W2_EARLY, E * WG):
                if k + 1 < E * WG:
                    scale_w2(k + 1)
                act.wait_ge(w2_scaled, k + 1 - W2_EARLY)
                w2_high_half(k, 1.0)

            def x_half(i):
                s = i[1] % 2
                act.wait_ge(xt_transposed, index(i, 1))
                wait(act, up_done, index(i, -1))
                nc.scalar.activation(xtp[:, s, 0, :, :], ps[:, 6 + s, 0:F].rearrange("p (k n) -> p k n", k=KT), ACT.Copy,
                                     scale=X_SCALE).then_inc(x_high, 1)

            def h_half(i):
                s = i[1] % 2
                act.wait_ge(biased, index(i, 1))
                wait(act, down_done, index(i, -1))
                nc.scalar.activation(hp[:, s, 0, :, :], hb[:, :].rearrange("p (f n) -> p f n", f=FT), ACT.Relu).then_inc(h_high, 1)

            def step(i):
                s = i[1] % 2
                if exists(ahead(i, 3)):
                    x_half(ahead(i, 3))
                if exists(ahead(i, 1)):
                    h_half(ahead(i, 1))
                act.wait_ge(down_done, index(i, 1))
                wait(act, added, index(i, -1) * 16)
                nc.scalar.activation(ysb[:, s, :], ps[:, 4 + s, 0:F], ACT.Copy, scale=gate_of[:, bass.ds(index(i), 1)]).then_inc(y_high, 1)

            act.wait_ge(map_ready, 1)
            x_half((0, 0))
            x_half((0, 1))
            x_half((0, 2))
            h_half((0, 0))
            each_tile(act, step)

        @block.vector
        def _(dve):
            steps = [0]

            def link(ins):
                dve.wait_ge(dve_step, mark(ins))

            def mark(ins):
                steps[0] += 1
                ins.then_inc(dve_step, 1)
                return steps[0]

            dve.sem_inc(masked, AHEAD)

            def layer_norm(src, dst, n, done, loaded):
                for t in range(T):
                    if loaded is not None and t in X_ENDS:
                        dve.wait_ge(loaded[X_ENDS.index(t)], 16)
                    last = nc.vector.bn_stats(stats[:, t, :], src[:, t, :])
                link(last)
                for t in range(T):
                    last = nc.vector.bn_aggr(mv[:, t, :], stats[:, t, :])
                link(last)
                nc.vector.tensor_scalar(rstd[:, :], mv[:, :, 1], LN_EPS, None, ALU.add).then_inc(var_ready, 1)
                dve.wait_ge(std_ready, n)
                link(nc.vector.reciprocal(rstd[:, :], rstd[:, :]))
                for t in range(T):
                    nc.vector.tensor_scalar(dst[:, t, :], src[:, t, :], mv[:, t, 0:1], rstd[:, t:t + 1],
                                            ALU.subtract, ALU.mult).then_inc(done, 1)

            layer_norm(xtm, xtm, 1, ln_done, x_loaded)
            dve.wait_ge(wv_made, 1)
            wv_ps = ps[:, 7, 0:KT * 2 * H].rearrange("p (k c) -> p k c", k=KT)
            nc.vector.tensor_copy(wv[:, :, :], wv_ps).then_inc(wv_copied, 1)
            for k in range(KT):
                nc.vector.tensor_copy(w_bd[:, k, P:P + 2], wv_ps[:, k, H + 2 * k:H + 2 * k + 2]).then_inc(wv_copied, 1)
            dve.wait_ge(consts_loaded, ALL_CONSTS)
            link(nc.vector.tensor_scalar(b2high, b2row, W_SCALE, None, ALU.mult))
            nc.vector.scalar_tensor_tensor(b2low, b2row, W_SCALE, b2high, ALU.mult, ALU.subtract).then_inc(b2_split, 2)
            for t in range(T):
                dve.wait_ge(xw_done, t + 1)
                xw_ps = ps[:, 4 + t % 3, 0:KT * (P + 2)].rearrange("p (k c) -> p k c", k=KT)
                nc.vector.tensor_copy(xw_tm[:, t, :].rearrange("p (k c) -> p k c", k=KT), xw_ps[:, :, 0:P])
                nc.vector.tensor_scalar(f2h[:, t * H:(t + 1) * H].rearrange("p (k c) -> p k c", k=KT), xw_ps[:, :, P:P + 2],
                                        0.5, None, ALU.mult).then_inc(xw_copied, 1)

            def mask_steps(gp, t0, t1):
                with dve.Fori(t0, t1) as t:
                    for s in range(2):
                        dve.wait_ge(exp_done, t * 2 + (gp * T + s + 2))
                        if gp % 2 == 0:
                            dve.wait_ge(mask_loaded[s], (t + (gp // 2 * (T // 2) + 1)) * 16)
                        dve.wait_ge(e_free, gp * T + t * 2 + s + 1)
                        nc.vector.tensor_tensor(
                            buf_e[:, s, :].rearrange("p (h n) -> p h n", h=2),
                            buf_p[:, s, :].rearrange("p (h n) -> p h n", h=2),
                            mask[:, bass.ds(t * 2 + s, 1), :].to_broadcast([P, 2, HALF]),
                            ALU.mult).then_inc(masked, 1)

            def invert(gp):
                i, times = inverse_by(gp)
                dve.wait_ge(den_moved[i], 32 * times)
                link(nc.vector.tensor_scalar(den[:, :], den[:, :], TINY, None, ALU.max))
                nc.vector.reciprocal(den[:, :], den[:, :]).then_inc(inv_ready, 1)

            def normalise(gp):
                i, times = inverse_by(gp)
                dve.wait_ge(inv_spread[i], 32 * times)
                half, pair = gp % PASSES // 2, gp % 2
                for h in range(2):
                    q = slice(h * D, (h + 1) * D)
                    nc.vector.tensor_tensor(xc[q, pair, half * HALF:(half + 1) * HALF], raw[q, h, :], invb[q, :],
                                            ALU.mult).then_inc(xc_ready, 1)

            def pass_stats(gp):
                for c in range(gp // 2 * NB, (gp // 2 + 1) * NB):
                    last = block_stats(xc, gp % 2, c)
                return last

            def attention(a):
                for q in range(PASSES):
                    gp = a * PASSES + q
                    if q:
                        mask_steps(gp, 0, 3)
                        invert(gp - 1)
                        mask_steps(gp, 3, 6)
                        normalise(gp - 1)
                        dve.wait_ge(xc_ready, 2 * gp)
                        if a == 0:
                            pass_stats(gp - 1)
                        mask_steps(gp, 6, T // 2)
                    else:
                        mask_steps(gp, 0, T // 2)
                    for b in range(2 * NB):
                        dve.wait_ge(bank_done, 2 * NB * gp + b + 1)
                        nc.vector.tensor_copy(raw[:, b // NB, b % NB * BLK:(b % NB + 1) * BLK], ps[:, b, 0:BLK]).then_inc(raw_copied, 1)
                invert(a * PASSES + PASSES - 1)
                if a == 1:
                    for k in range(WG):
                        w1_low_half(k)
                normalise(a * PASSES + PASSES - 1)

            def block_stats(src, k, c):
                return nc.vector.bn_stats(bnst[:, k, c, :], src[:, k, c * BLK:min((c + 1) * BLK, N)])

            def batch_norm(n, src, g, b):
                for k in range(KT):
                    last = nc.vector.bn_aggr(bnmv[:, k, :], bnst[:, k, :, :].rearrange("p a b -> p (a b)"))
                link(last)
                nc.vector.tensor_scalar(bnsc[:, :, 0], bnmv[:, :, 1], BN_EPS, None, ALU.add).then_inc(var_ready, 1)
                dve.wait_ge(std_ready, n)
                link(nc.vector.reciprocal(bnsc[:, :, 1], bnsc[:, :, 0]))
                link(nc.vector.tensor_tensor(bnsc[:, :, 2], bnsc[:, :, 1], vecs[:, g, :], ALU.mult))
                link(nc.vector.tensor_tensor(bnsc[:, :, 1], bnsc[:, :, 2], bnmv[:, :, 0], ALU.mult))
                link(nc.vector.tensor_tensor(bnsc[:, :, 3], vecs[:, b, :], bnsc[:, :, 1], ALU.subtract))
                for c in range(BN_PARTS):
                    cols = slice(c * BN_COLS, (c + 1) * BN_COLS)
                    for k in range(KT):
                        nc.vector.tensor_scalar(src[:, k, cols], src[:, k, cols],
                                                bnsc[:, k, 2:3], bnsc[:, k, 3:4], ALU.mult, ALU.add).then_inc(bn_applied, 1)

            def w1_low_half(k):
                src, high, low = w_piece(w1p, k)
                dve.wait_ge(w1_high, k + 1)
                nc.vector.scalar_tensor_tensor(low, src, W_SCALE, high, ALU.mult, ALU.subtract).then_inc(w1_low, 1)

            def elu_sum(n, m, b):
                cols = slice(b * BLK, (b + 1) * BLK)
                dve.wait_ge(elu_relu, n + 1)
                return mark(nc.vector.scalar_tensor_tensor(buf_p[:, m, cols], buf_s[:, m, cols], 1.0, buf_p[:, m, cols], ALU.min, ALU.add))

            def elu(summed, m, b, dst, res):
                cols = slice(b * BLK, (b + 1) * BLK)
                dve.wait_ge(dve_step, summed)
                if res is None:
                    nc.vector.tensor_scalar(dst[:, m, cols], buf_p[:, m, cols], -1.0, None, ALU.add).then_inc(h_done, 1)
                else:
                    nc.vector.scalar_tensor_tensor(dst[:, m, cols], buf_p[:, m, cols], -1.0, res[:, m, cols], ALU.add, ALU.add).then_inc(h_done, 1)

            attention(0)
            dve.wait_ge(xc_ready, 2 * PASSES)
            link(pass_stats(PASSES - 1))
            batch_norm(2, xc, ENC_G, ENC_B)
            for u in range(UNITS):
                m, b = u // BLOCKS, u % BLOCKS
                summed = elu_sum(u, m, b)
                if u:
                    dve.wait_ge(h_done, u)
                    block_stats(buf_e, (u - 1) // BLOCKS, (u - 1) % BLOCKS)
                elu(summed, m, b, buf_e, xc)
            dve.wait_ge(h_done, UNITS)
            link(block_stats(buf_e, KT - 1, BLOCKS - 1))
            batch_norm(3, buf_e, EM_G, EM_B)
            attention(1)
            pieces, unit = WG, None
            for n, (which, m, b) in enumerate(decoder):
                summed = elu_sum(UNITS + n, m, b)
                if which == 2:
                    w1_low_half(pieces)
                    pieces += 1
                if unit:
                    dve.wait_ge(h_done, unit[0])
                    block_stats(xc, unit[1], unit[2])
                elu(summed, m, b, buf_e if which == 1 else xc, None if which == 1 else buf_e)
                unit = (UNITS + n + 1, m, b) if which == 2 else None
            dve.wait_ge(h_done, unit[0])
            link(block_stats(xc, unit[1], unit[2]))
            batch_norm(4, xc, DM_G, DM_B)
            dve.wait_ge(res_loaded, 16)
            for t in range(T):
                dve.wait_ge(ot_done, t + 1)
                last = nc.vector.tensor_tensor(x1[:, t, :], x1[:, t, :], ps[:, t % 8, 0:F], ALU.add).then_inc(x1_done, 1)
            dve.wait_ge(x1_done, T)
            layer_norm(x1, ptm, 5, ln2_done, None)
            for k in range(E * WG - WG - UNITS):
                w1_low_half(WG + UNITS + k)
                if k < W2_EARLY:
                    src, high, low = w_piece(w2p, k)
                    dve.wait_ge(w2_high, k + 1)
                    nc.vector.scalar_tensor_tensor(low, src, W_SCALE, high, ALU.mult, ALU.subtract).then_inc(w2_low, 1)
            dve.wait_ge(lg_done, 1)
            link(nc.vector.tensor_tensor(logits[:, :, :], ps[:, 7, 0:T * E].rearrange("p (t e) -> p t e", e=E),
                                         bg_sb[:, :].rearrange("p (a e) -> p a e", a=1).to_broadcast([P, T, E]), ALU.add))
            for t in range(T):
                last = nc.vector.max(top[:, t, :], logits[:, t, :])
            link(last)
            for t in range(T):
                last = nc.vector.max_index(topi[:, t, :], top[:, t, :], logits[:, t, :])
            link(last)
            nc.vector.tensor_copy(topf[:, :, :], topi[:, :, 0:2])
            nc.vector.tensor_tensor(gate[:, 0, :], top[:, :, 1], top[:, :, 0], ALU.subtract).then_inc(gate_in, 1)
            dve.wait_ge(gate_exp, 1)
            link(nc.vector.tensor_scalar(gate[:, 2, :], gate[:, 1, :], 1.0, None, ALU.add))
            link(nc.vector.reciprocal(gate[:, 2, :], gate[:, 2, :]))
            link(nc.vector.tensor_tensor(gate[:, 3, :], gate[:, 2, :], gate[:, 1, :], ALU.mult))
            dve.wait_ge(tri_made, 3)
            for k in range(2):
                last = nc.vector.tensor_tensor(hot[:, k, :, :], count[:, 0:E].rearrange("p (a e) -> p a e", a=1).to_broadcast([P, T, E]),
                                               topf[:, :, k:k + 1].to_broadcast([P, T, E]), ALU.is_equal)
            link(last)
            nc.vector.tensor_tensor(both[:, :, :], hot[:, 0, :, :], hot[:, 1, :, :], ALU.add).then_inc(hot_ready, 1)
            dve.wait_ge(pos_done, 1)
            totals = ps[:, 5, 0:T * E].rearrange("p (t e) -> p t e", e=E)
            ranks = ps[:, 4, 0:T * E].rearrange("p (t e) -> p t e", e=E)
            link(nc.vector.tensor_copy(pre[:, 0, :, :], totals))
            cur, d = 0, 1
            while d < T:
                nc.vector.tensor_copy(pre[:, 1 - cur, 0:d, :], pre[:, cur, 0:d, :])
                link(nc.vector.tensor_tensor(pre[:, 1 - cur, d:T, :], pre[:, cur, d:T, :], pre[:, cur, 0:T - d, :], ALU.add))
                cur, d = 1 - cur, 2 * d
            TILES, SUM, FIRST = 0, 1, 3
            full = ps[:, 3, 0:E * T].rearrange("p (e m) -> p e m", e=E)
            past = ps[:, 2, 0:S * E].rearrange("p (s e) -> p s e", e=E)
            eid_f = ps[:, 1, 0:S]
            link(nc.vector.tensor_scalar(ends[:, 5, :], pre[:, cur, T - 1, :], 1.0 / P, None, ALU.mult))
            link(nc.vector.tensor_tensor(full, ends[:, 5, :].rearrange("p (e a) -> p e a", a=1).to_broadcast([P, E, T]),
                                         count[:, 0:T].rearrange("p (a m) -> p a m", a=1).to_broadcast([P, E, T]), ALU.is_gt))
            link(nc.vector.tensor_reduce(ends[:, TILES, :], full, mybir.AxisListType.X, ALU.add))
            link(nc.vector.tensor_copy(ends[:, SUM, :], ends[:, TILES, :]))
            at, d = SUM, 1
            while d < E:
                to = SUM + 1 if at == SUM else SUM
                nc.vector.tensor_copy(ends[:, to, 0:d], ends[:, at, 0:d])
                link(nc.vector.tensor_tensor(ends[:, to, d:E], ends[:, at, d:E], ends[:, at, 0:E - d], ALU.add))
                at, d = to, 2 * d
            link(nc.vector.tensor_tensor(ends[:, FIRST, :], ends[:, at, :], ends[:, TILES, :], ALU.subtract))
            link(nc.vector.tensor_scalar(ends[:, FIRST + 1, :], ends[:, FIRST, :], float(P), None, ALU.mult))
            link(nc.vector.tensor_tensor(pre[:, cur, :, :], pre[:, cur, :, :], totals, ALU.subtract))
            link(nc.vector.tensor_tensor(pre[:, cur, :, :], pre[:, cur, :, :], ranks, ALU.add))
            link(nc.vector.tensor_tensor(pre[:, cur, :, :], pre[:, cur, :, :],
                                         ends[:, FIRST + 1, :].rearrange("p (a e) -> p a e", a=1).to_broadcast([P, T, E]), ALU.add))
            for k in range(2):
                link(nc.vector.tensor_tensor(pre[:, 1 - cur, :, :], pre[:, cur, :, :], hot[:, k, :, :], ALU.mult))
                link(nc.vector.tensor_reduce(slot[:, k * T:(k + 1) * T], pre[:, 1 - cur, :, :], mybir.AxisListType.X, ALU.add))
            link(nc.vector.tensor_copy(slot_i[:, 0, :], slot[:, :]))
            nc.vector.tensor_scalar(slot_i[:, 1, :], slot_i[:, 0, :], P - 1, None, ALU.bitwise_and)
            link(nc.vector.tensor_scalar(slot_i[:, 2, :], slot_i[:, 0, :], P.bit_length() - 1, None, ALU.logical_shift_right))
            link(nc.vector.tensor_copy(place[:, :, :], slot_i[:, 1:3, :]))
            link(nc.vector.tensor_tensor(past, count[:, 0:S].rearrange("p (s a) -> p s a", a=1).to_broadcast([P, S, E]),
                                         ends[:, at, :].rearrange("p (a e) -> p a e", a=1).to_broadcast([P, S, E]), ALU.is_ge))
            link(nc.vector.tensor_reduce(eid_f, past, mybir.AxisListType.X, ALU.add))
            link(nc.vector.tensor_scalar(eid_f, eid_f, float(E - 1), None, ALU.min))
            packed = free[:, :]
            link(nc.vector.tensor_copy(packed, eid_f))
            for k in range(1, PACKED):
                link(nc.vector.scalar_tensor_tensor(packed[:, 0:S - k], eid_f[:, k:S], float(E ** k), packed[:, 0:S - k], ALU.mult, ALU.add))
            nc.vector.tensor_copy(eids[:, :], packed).then_inc(slots_ready, 1)
            nc.vector.tensor_scalar(b1s[:, :, :], b1_sb[:, :, :], H_SCALE, None, ALU.mult).then_inc(b1_scaled, 1)
            nodes = node[:, :, :].rearrange("p k t -> p (k t)")
            gates = gate[:, 2:4, :].rearrange("p k t -> p (k t)")
            dve.wait_ge(xn_stored, 32)
            for c in range(PAIRS // CHUNK):
                part = slice(c * CHUNK, (c + 1) * CHUNK)

                def spread(a, n):
                    return a.rearrange("p (c a) -> p c a", a=1).to_broadcast([P, CHUNK, n])

                if c >= 2:
                    dve.wait_ge(hots_used, c - 1)
                nc.vector.tensor_tensor(col_hot[:, c % 2, :, :], spread(place[:, 0, part], P),
                                        count[:, :].rearrange("p (a n) -> p a n", a=1).to_broadcast([P, CHUNK, P]), ALU.is_equal)
                link(nc.vector.tensor_tensor(tile_hot[:, c % 2, :, 0, :], spread(place[:, 1, part], S),
                                             count[:, 0:S].rearrange("p (a n) -> p a n", a=1).to_broadcast([P, CHUNK, S]), ALU.is_equal))
                nc.vector.tensor_tensor(tile_hot[:, c % 2, :, 1, :], tile_hot[:, c % 2, :, 0, :], spread(nodes[:, part], S), ALU.mult)
                nc.vector.tensor_tensor(tile_hot[:, c % 2, :, 2, :], tile_hot[:, c % 2, :, 0, :], spread(gates[:, part], S), ALU.mult).then_inc(hots_made, 1)
            dve.wait_ge(hots_used, PAIRS // CHUNK)
            dve.wait_ge(small_free, 6)
            link(nc.vector.tensor_scalar(free[:, :], ps[:, 0, 0:S], spare[:, 1:2], spare[:, 0:1], ALU.mult, ALU.add))
            nc.vector.tensor_tensor(node_of[:, :], free[:, :], ps[:, 0, S:2 * S], ALU.add)
            nc.vector.tensor_scalar(gate_of[:, :], ps[:, 0, 2 * S:3 * S], 1.0 / Y_SCALE, None, ALU.mult).then_inc(map_ready, 1)
            def x_half(i):
                s = i[1] % 2
                dve.wait_ge(x_high, index(i, 1))
                nc.vector.scalar_tensor_tensor(xtp[:, s, 1, :, :].rearrange("p k n -> p (k n)"), ps[:, 6 + s, 0:F], X_SCALE,
                                               xtp[:, s, 0, :, :].rearrange("p k n -> p (k n)"), ALU.mult, ALU.subtract).then_inc(x_low, 1)

            def add_bias(i):
                s = i[1] % 2
                e = nc.vector.value_load(eids[0:1, bass.ds(index(i), 1)], min_val=0, max_val=E ** PACKED - 1) & (E - 1)
                dve.wait_ge(up_done, index(i, 1))
                wait(dve, h_low, index(i))
                nc.vector.tensor_tensor(hb[:, :].rearrange("p (f n) -> p f n", f=FT),
                                        ps[:, 2 * s:2 * s + 2, :].rearrange("p b (f n) -> p (b f) n", n=P),
                                        b1s[:, bass.ds(e, 1), :].rearrange("p a f -> p (a f)").rearrange("p (f a) -> p f a", a=1).to_broadcast([P, FT, P]),
                                        ALU.add).then_inc(biased, 1)

            def h_half(i):
                s = i[1] % 2
                dve.wait_ge(h_high, index(i, 1))
                nc.vector.scalar_tensor_tensor(hp[:, s, 1, :, :].rearrange("p f n -> p (f n)"), hb[:, :], 0.0,
                                               hp[:, s, 0, :, :].rearrange("p f n -> p (f n)"), ALU.max, ALU.subtract).then_inc(h_low, 1)

            def add_y(i):
                s = i[1] % 2
                dve.wait_ge(y_high, index(i, 1))
                nc.vector.scalar_tensor_tensor(ysb[:, s, :], ps[:, 4 + s, F:2 * F], gate_of[:, bass.ds(index(i), 1)], ysb[:, s, :],
                                               ALU.mult, ALU.add).then_inc(y_copied, 1)

            def step(i):
                if exists(ahead(i, 1)):
                    add_bias(ahead(i, 1))
                if exists(ahead(i, -1)):
                    add_y(ahead(i, -1))
                if exists(ahead(i, 3)):
                    x_half(ahead(i, 3))
                if exists(ahead(i, 1)):
                    h_half(ahead(i, 1))

            dve.wait_ge(slots_ready, 1)
            dve.wait_ge(b1_scaled, 1)
            x_half((0, 0))
            x_half((0, 1))
            add_bias((0, 0))
            x_half((0, 2))
            h_half((0, 0))
            each_tile(dve, step)
            add_y((0, S - 1))
        @block.tensor
        def _(pe):
            pe.sem_inc(e_free, AHEAD)
            pe.wait_ge(ident_made, 1)

            def transposes(src, ready, done, copied):
                for t in range(T):
                    pe.wait_ge(ready, t + 1)
                    if t >= 4:
                        pe.wait_ge(copied, t - 3)
                    for k in range(KT):
                        last = nc.tensor.transpose(ps[:, t % 4, k * P:(k + 1) * P], src[:, t, k * P:(k + 1) * P], ident[:, :])
                    last.then_inc(done, 1)

            transposes(xtm, ln_done, tr_done, tr_copied)
            pe.wait_ge(consts_loaded, ALL_CONSTS)
            for k in range(KT):
                last = nc.tensor.matmul(ps[:, 7, k * 2 * H:(k + 1) * 2 * H], wt_bd[:, k, :], v_bd[:, k, :], start=True, stop=True)
            last.then_inc(wv_made, 1)
            pe.wait_ge(wv_copied, 1 + KT)
            pe.wait_ge(tr_copied, T)
            for b in range(BLOCKS):
                if b >= 4:
                    pe.wait_ge(f1_copied, b - 3)
                for k in range(KT):
                    last = nc.tensor.matmul(ps[0:H, b % 4, 0:BLK], wv[:, k, 0:H], buf_e[:, k, b * BLK:(b + 1) * BLK],
                                            start=(k == 0), stop=(k == KT - 1))
                last.then_inc(f1_done, 1)
            for t in range(T):
                if t >= 3:
                    pe.wait_ge(xw_copied, t - 2)
                for k in range(KT):
                    last = nc.tensor.matmul(ps[:, 4 + t % 3, k * (P + 2):(k + 1) * (P + 2)], buf_e[:, k, t * P:(t + 1) * P], w_bd[:, k, :],
                                            start=True, stop=True)
                last.then_inc(xw_done, 1)

            def product(gp, t, s, first, last_step):
                pe.wait_ge(masked, t * 2 + (gp * T + s + 1 + AHEAD))
                pe.wait_ge(stage_loaded[s], (t + (gp * (T // 2) + 1)) * 16)
                for h in range(2):
                    for b in range(NB):
                        if first and gp:
                            pe.wait_ge(raw_copied, 2 * NB * (gp - 1) + h * NB + b + 1)
                        mm = nc.tensor.matmul(ps[:, h * NB + b, 0:BLK], stage[:, s, h * D:h * D + P],
                                              buf_e[:, s, h * HALF + b * BLK:h * HALF + (b + 1) * BLK],
                                              start=first, stop=last_step)
                        if last_step:
                            mm.then_inc(bank_done, 1)
                if last_step:
                    pe.wait_ge(bank_done, 2 * NB * (gp + 1))
                    pe.sem_inc(e_free, 1)
                else:
                    mm.then_inc(e_free, 1)

            def attention(a):
                for q in range(PASSES):
                    gp = a * PASSES + q
                    product(gp, 0, 0, True, False)
                    product(gp, 0, 1, False, False)
                    with pe.Fori(1, T // 2 - 1) as t:
                        product(gp, t, 0, False, False)
                        product(gp, t, 1, False, False)
                    product(gp, T // 2 - 1, 0, False, False)
                    product(gp, T // 2 - 1, 1, False, True)

            attention(0)
            pe.wait_ge(raw_copied, 2 * NB * PASSES)
            for u in range(UNITS):
                m, b = u // BLOCKS, u % BLOCKS
                if m == 0:
                    pe.wait_ge(bn_applied, applied(0, (b + 1) * BLK))
                if u >= 8:
                    pe.wait_ge(elu_relu, u - 7)
                for k in range(KT):
                    mm = nc.tensor.matmul(ps[:, u % 8, 0:BLK], emw_sb[:, k, m * P:(m + 1) * P], xc[:, k, b * BLK:(b + 1) * BLK],
                                          start=(k == 0), stop=(k == KT - 1))
                mm.then_inc(z_done, 1)
            for t in range(T // 2):
                pe.wait_ge(bn_applied, applied(1, (2 * t + 2) * P))
                if t < 8:
                    pe.wait_ge(elu_relu, UNITS)
                else:
                    pe.wait_ge(et_copied, t - 7)
                for i in range(2):
                    for k in range(KT):
                        last = nc.tensor.transpose(ps[:, t % 8, i * F + k * P:i * F + (k + 1) * P],
                                                   buf_e[:, k, (2 * t + i) * P:(2 * t + i + 1) * P], ident[:, :])
                last.then_inc(et_done, 1)
            pe.wait_ge(et_copied, T // 2)
            attention(1)
            pe.wait_ge(raw_copied, 4 * NB * PASSES)
            pe.wait_ge(xc_ready, 4 * PASSES)
            for n, (which, m, b) in enumerate(decoder):
                if n >= 8:
                    pe.wait_ge(elu_relu, UNITS + n - 7)
                cols = slice(b * BLK, (b + 1) * BLK)
                if which == 1:
                    mm = nc.tensor.matmul(ps[:, n % 8, 0:BLK], wt_bd[:, m, :], xc[:, m, cols], start=True, stop=True)
                else:
                    pe.wait_ge(h_done, UNITS + decoder.index((1, KT - 1, b)) + 1)
                    for k in range(KT):
                        mm = nc.tensor.matmul(ps[:, n % 8, 0:BLK], dmw_sb[:, k, m * P:(m + 1) * P], buf_e[:, k, cols],
                                              start=(k == 0), stop=(k == KT - 1))
                mm.then_inc(z_done, 1)
            pe.wait_ge(elu_relu, 3 * UNITS)
            for t in range(T):
                pe.wait_ge(bn_applied, applied(2, (t + 1) * P))
                if t >= 8:
                    pe.wait_ge(x1_done, t - 7)
                for k in range(KT):
                    last = nc.tensor.transpose(ps[:, t % 8, k * P:(k + 1) * P], xc[:, k, t * P:(t + 1) * P], ident[:, :])
                last.then_inc(ot_done, 1)
            pe.wait_ge(x1_done, T)
            transposes(ptm, ln2_done, tr2_done, tr2_copied)
            pe.wait_ge(tr2_copied, T)
            for t in range(T):
                for k in range(KT):
                    last = nc.tensor.matmul(ps[:, 7, t * E:(t + 1) * E], buf_e[:, k, t * P:(t + 1) * P], wg_sb[:, k, :],
                                            start=(k == 0), stop=(k == KT - 1))
            last.then_inc(lg_done, 1)
            pe.wait_ge(tri_made, 3)
            pe.wait_ge(hot_ready, 1)
            nc.tensor.matmul(ps[:, 4, 0:T * E], before[:, :], both[:, :, :].rearrange("p t e -> p (t e)"), start=True, stop=True)
            nc.tensor.matmul(ps[:, 5, 0:T * E], ones[:, :], both[:, :, :].rearrange("p t e -> p (t e)"), start=True, stop=True).then_inc(pos_done, 1)
            for c in range(PAIRS // CHUNK):
                pe.wait_ge(hots_made, c + 1)
                for i in range(CHUNK):
                    n = c * CHUNK + i
                    last = nc.tensor.matmul(ps[:, 0, 0:3 * S], col_hot[:, c % 2, i, :],
                                            tile_hot[:, c % 2, i, :, :].rearrange("p a s -> p (a s)"), start=(n == 0), stop=(n == PAIRS - 1))
                last.then_inc(hots_used, 1)

            def transpose_x(i):
                s = i[1] % 2
                pe.wait_ge(xt_loaded[i[1] % XRING], rounds(i, XRING, 1) * 16)
                wait(pe, x_low, index(i, -1))
                for k in range(KT):
                    last = nc.tensor.transpose(ps[:, 6 + s, k * P:(k + 1) * P], xt[:, i[1] % XRING, k * P:(k + 1) * P], ident[:, :])
                last.then_inc(xt_transposed, 1)

            HALVES = ((0, 0), (0, 1), (1, 0))

            words, experts = {}, {}

            def load_experts(i, count):
                words.clear()
                experts.clear()
                for k in range(count):
                    if k % PACKED == 0:
                        word = nc.tensor.value_load(eids[0:1, bass.ds(index(i, k), 1)], min_val=0, max_val=E ** PACKED - 1)
                    words[i[1] + k] = word, E_BITS * (k % PACKED)

            def expert(i):
                if i[1] not in experts:
                    word, bit = words[i[1]]
                    experts[i[1]] = nc.snap((word >> bit) & (E - 1))
                return experts[i[1]]

            def up(i, e, f, k):
                s = i[1] % 2
                for n, (a, b) in enumerate(HALVES):
                    g = k * (WG // KT) + f // 4
                    mm = nc.tensor.matmul(ps[:, 2 * s + f // 4, f % 4 * P:(f % 4 + 1) * P],
                                          w1p[:, bass.ds(e * WG + g, 1), a * GRAN + f % 4 * P:a * GRAN + (f % 4 + 1) * P]
                                          .rearrange("p a c -> p (a c)"),
                                          xtp[:, s, b, k, :], start=(n == 0 and k == 0), stop=(n == 2 and k == KT - 1))
                if f == FT - 1 and k == KT - 1:
                    mm.then_inc(up_done, 1)

            def down(i, e, f, b):
                s = i[1] % 2
                cols = F if b else 2 * F
                mm = nc.tensor.matmul(ps[:, 4 + s, 0:cols], hp[:, s, b, f, :],
                                      w2p[:, bass.ds(e * WG + f // 2 + 1, 1), f % 2 * 2 * F:f % 2 * 2 * F + cols]
                                      .rearrange("p a c -> p (a c)"),
                                      start=(f == 0 and b == 0), stop=(f == FT - 1 and b == 0))
                if b == 0 and f == FT - 1:
                    mm.then_inc(down_done, 1)

            def step(i):
                s, j = i[1] % 2, ahead(i, 2)
                if exists(ahead(i, 3)):
                    transpose_x(ahead(i, 3))
                e_down = expert(i)
                if exists(j):
                    e_up = expert(j)
                    pe.wait_ge(x_low, index(j, 1))
                    pe.wait_ge(biased, index(j, -1))
                pe.wait_ge(h_low, index(i, 1))
                wait(pe, y_copied, index(i, -1))
                for f in range(FT):
                    order = (1, 0) if f == FT - 1 else (0, 1)
                    for k in range(KT):
                        if exists(j):
                            up(j, e_up, f, k)
                        down(i, e_down, f, order[k])
                    if f == 0:
                        nc.tensor.matmul(ps[:, 4 + s, 0:F], ones2[:, :], b2p[:, bass.ds(e_down * F, F)], start=False, stop=False)

            pe.wait_ge(slots_ready, 1)
            pe.wait_ge(map_ready, 1)
            pe.wait_ge(b2_loaded, 16)
            pe.wait_ge(w1_low, E * WG)
            pe.wait_ge(w2_low, E * WG)
            transpose_x((0, 0))
            transpose_x((0, 1))
            load_experts((0, 0), 2)
            for c in range(2):
                if c == 1:
                    transpose_x((0, 2))
                pe.wait_ge(x_low, c + 1)
                for f in range(FT):
                    for k in range(KT):
                        up((0, c), expert((0, c)), f, k)
            each_tile(pe, step, load_experts)


_OUT = ("out_dram", (NP + P, F))


def kernel(x, adj, L0_gnn_W, L0_gnn_V, L0_gnn_enc_bn_gamma, L0_gnn_enc_bn_beta, L0_gnn_enc_mlp_W, L0_gnn_enc_mlp_b,
           L0_gnn_enc_mlp_bn_gamma, L0_gnn_enc_mlp_bn_beta, L0_gnn_dec_mlp_W, L0_gnn_dec_mlp_b,
           L0_gnn_dec_mlp_bn_gamma, L0_gnn_dec_mlp_bn_beta, L0_ffn_Wg, L0_ffn_bg, L0_ffn_W1, L0_ffn_b1,
           L0_ffn_W2, L0_ffn_b2):
    import numpy as np
    import concourse.bacc as bacc
    from concourse.bass_utils import run_bass_kernel_spmd

    xp = np.zeros((NP, F), np.float32)
    xp[:N] = np.asarray(x)
    adj_t = np.zeros((NP, NP), np.float32)
    adj_t[:N, :N] = np.asarray(adj).T
    w = np.asarray(L0_gnn_W)
    host = {
        "x": xp, "adj_t": adj_t, "w": w, "wt": w.transpose(0, 2, 1), "v": L0_gnn_V,
        "enc_g": L0_gnn_enc_bn_gamma, "enc_b": L0_gnn_enc_bn_beta,
        "emw_t": np.asarray(L0_gnn_enc_mlp_W).T, "emb": L0_gnn_enc_mlp_b,
        "em_g": L0_gnn_enc_mlp_bn_gamma, "em_b": L0_gnn_enc_mlp_bn_beta,
        "dmw_t": np.asarray(L0_gnn_dec_mlp_W).T, "dmb": L0_gnn_dec_mlp_b,
        "dm_g": L0_gnn_dec_mlp_bn_gamma, "dm_b": L0_gnn_dec_mlp_bn_beta,
        "wg": L0_ffn_Wg, "bg": L0_ffn_bg, "w1": L0_ffn_W1, "b1": L0_ffn_b1, "w2": L0_ffn_W2, "b2": L0_ffn_b2,
    }
    nc = bacc.Bacc("TRN2", target_bir_lowering=False, num_devices=1)
    arrays, args = {}, {}
    for name, a in host.items():
        a = np.ascontiguousarray(np.asarray(a))
        arrays[f"in_{name}"] = a
        args[name] = nc.dram_tensor(f"in_{name}", a.shape, mybir.dt.from_np(a.dtype), kind="ExternalInput").ap()
    out = nc.dram_tensor(_OUT[0], _OUT[1], F32, kind="ExternalOutput").ap()
    build(nc, out=out, **args)
    r = run_bass_kernel_spmd(nc, [arrays], core_ids=[0])
    return r.results[0][_OUT[0]][:N]
```
